# Optimizing a Trainium2 kernel written in Bass

```python
import numpy as np
import jax
import jax.numpy as jnp

def _softmax(x, axis=-1):
    return jax.nn.softmax(x, axis=axis)

def _gelu(x):
    return jax.nn.gelu(x, approximate=True)

def _silu(x):
    return jax.nn.silu(x)

def _sigmoid(x):
    return jax.nn.sigmoid(x)

def _layernorm(x, axis=-1, eps=1e-05):
    m = jnp.mean(x, axis=axis, keepdims=True)
    v = jnp.var(x, axis=axis, keepdims=True)
    return (x - m) / jnp.sqrt(v + eps)

def _scatter_add(tgt, idx, src, axis=0):
    return tgt.at[idx].add(src)

def _segment_sum(src, seg, n):
    return jax.ops.segment_sum(src, seg, n)
kernel_name = 'mk_seq_postln_d1_jaxref_r8_8d2cf5'

def setup_inputs(seed: int=0):
    np.random.seed(seed)
    _w = jnp.asarray

    def _L0_attn_setup():
        import jax, jax.numpy as jnp
        import numpy as np
        B, S, D = (1, 512, 128)
        H, KV, WIN = (8, 2, 32)
        HD = D // H
        FP16_MIN = -65504.0
        key = jax.random.key(seed)
        ks = jax.random.split(key, 10)
        sc = 0.02
        return {'x': jax.random.normal(ks[0], (B, S, D), dtype=jnp.float32), 'sink_bias': jnp.float32(0.0), 'Wq': jax.random.normal(ks[1], (H * HD, D), dtype=jnp.float32) * sc, 'bq': jnp.zeros((H * HD,), dtype=jnp.float32), 'Wk': jax.random.normal(ks[2], (KV * HD, D), dtype=jnp.float32) * sc, 'bk': jnp.zeros((KV * HD,), dtype=jnp.float32), 'Wv': jax.random.normal(ks[3], (KV * HD, D), dtype=jnp.float32) * sc, 'bv': jnp.zeros((KV * HD,), dtype=jnp.float32), 'Wo': jax.random.normal(ks[4], (D, H * HD), dtype=jnp.float32) * sc, 'bo': jnp.zeros((D,), dtype=jnp.float32)}
    _L0_attn_in = _L0_attn_setup()

    def _L0_ffn_setup():
        import jax, jax.numpy as jnp
        import numpy as np
        D_MODEL = 128
        HIDDEN = 256
        N_EXPERTS = 8
        TOP_K = 2
        key = jax.random.key(seed)
        ks = jax.random.split(key, 9)
        s = 0.02
        x = jax.random.normal(ks[0], (4, 256, D_MODEL), dtype=jnp.float32)
        sw1 = jax.random.normal(ks[1], (D_MODEL, HIDDEN), dtype=jnp.float32) * s
        sw2 = jax.random.normal(ks[2], (D_MODEL, HIDDEN), dtype=jnp.float32) * s
        sw3 = jax.random.normal(ks[3], (HIDDEN, D_MODEL), dtype=jnp.float32) * s
        ew1 = jax.random.normal(ks[4], (N_EXPERTS, D_MODEL, HIDDEN), dtype=jnp.float32) * s
        ew2 = jax.random.normal(ks[5], (N_EXPERTS, D_MODEL, HIDDEN), dtype=jnp.float32) * s
        ew3 = jax.random.normal(ks[6], (N_EXPERTS, HIDDEN, D_MODEL), dtype=jnp.float32) * s
        rw = jax.random.normal(ks[7], (D_MODEL, N_EXPERTS), dtype=jnp.float32) * s
        rb = jax.random.normal(ks[8], (N_EXPERTS,), dtype=jnp.float32) * s
        return {'x': x, 'sw1': sw1, 'sw2': sw2, 'sw3': sw3, 'ew1': ew1, 'ew2': ew2, 'ew3': ew3, 'rw': rw, 'rb': rb}
    _L0_ffn_in = _L0_ffn_setup()
    _d = {'L0_attn_x': _L0_attn_in['x'], 'L0_attn_sink_bias': _L0_attn_in['sink_bias'], 'L0_attn_Wq': _L0_attn_in['Wq'], 'L0_attn_bq': _L0_attn_in['bq'], 'L0_attn_Wk': _L0_attn_in['Wk'], 'L0_attn_bk': _L0_attn_in['bk'], 'L0_attn_Wv': _L0_attn_in['Wv'], 'L0_attn_bv': _L0_attn_in['bv'], 'L0_attn_Wo': _L0_attn_in['Wo'], 'L0_attn_bo': _L0_attn_in['bo'], 'L0_ffn_sw1': _L0_ffn_in['sw1'], 'L0_ffn_sw2': _L0_ffn_in['sw2'], 'L0_ffn_sw3': _L0_ffn_in['sw3'], 'L0_ffn_ew1': _L0_ffn_in['ew1'], 'L0_ffn_ew2': _L0_ffn_in['ew2'], 'L0_ffn_ew3': _L0_ffn_in['ew3'], 'L0_ffn_rw': _L0_ffn_in['rw'], 'L0_ffn_rb': _L0_ffn_in['rb']}
    _x0 = _d['L0_attn_x']
    _d['L0_attn_x'] = jax.random.normal(jax.random.fold_in(jax.random.key(seed), 1), (2, 1024, 128), dtype=_x0.dtype)
    del _x0
    return _d

def reference(L0_attn_x, L0_attn_sink_bias, L0_attn_Wq, L0_attn_bq, L0_attn_Wk, L0_attn_bk, L0_attn_Wv, L0_attn_bv, L0_attn_Wo, L0_attn_bo, L0_ffn_sw1, L0_ffn_sw2, L0_ffn_sw3, L0_ffn_ew1, L0_ffn_ew2, L0_ffn_ew3, L0_ffn_rw, L0_ffn_rb):

    def _L0_attn_ref(x, sink_bias, Wq, bq, Wk, bk, Wv, bv, Wo, bo):
        import jax, jax.numpy as jnp
        import numpy as np
        B, S, D = (1, 512, 128)
        H, KV, WIN = (8, 2, 32)
        HD = D // H
        FP16_MIN = -65504.0
        b, s, d = x.shape
        q = (x @ Wq.T + bq).reshape(b, s, H, HD).transpose(0, 2, 1, 3)
        k = (x @ Wk.T + bk).reshape(b, s, KV, HD).transpose(0, 2, 1, 3)
        v = (x @ Wv.T + bv).reshape(b, s, KV, HD).transpose(0, 2, 1, 3)
        k = jnp.repeat(k, H // KV, axis=1)
        v = jnp.repeat(v, H // KV, axis=1)
        scores = jnp.einsum('bhqd,bhkd->bhqk', q, k) / jnp.sqrt(jnp.float32(HD))
        i = jnp.arange(s)[:, None]
        j = jnp.arange(s)[None, :]
        mask = (j <= i) & (j > i - WIN)
        scores = jnp.where(mask, scores, FP16_MIN)
        m = jnp.maximum(scores.max(axis=-1, keepdims=True), sink_bias)
        e = jnp.exp(scores - m)
        sink = jnp.exp(sink_bias - m)
        attn = e / (e.sum(axis=-1, keepdims=True) + sink)
        out = jnp.einsum('bhqk,bhkd->bhqd', attn, v)
        out = out.transpose(0, 2, 1, 3).reshape(b, s, H * HD)
        return out @ Wo.T + bo

    def _L0_ffn_ref(x, sw1, sw2, sw3, ew1, ew2, ew3, rw, rb):
        import jax, jax.numpy as jnp
        import numpy as np
        D_MODEL = 128
        HIDDEN = 256
        N_EXPERTS = 8
        TOP_K = 2
        shared = jnp.einsum('bth,hd->btd', jax.nn.silu(jnp.einsum('btd,dh->bth', x, sw1)) * jnp.einsum('btd,dh->bth', x, sw2), sw3)
        probs = jax.nn.softmax(jnp.einsum('btd,de->bte', x, rw) + rb, axis=-1)
        w, idx = jax.lax.top_k(probs, TOP_K)
        w = w / jnp.sum(w, axis=-1, keepdims=True)
        gates = jnp.sum(w[..., None] * jax.nn.one_hot(idx, N_EXPERTS, dtype=x.dtype), axis=-2)
        h = jax.nn.silu(jnp.einsum('btd,edh->beth', x, ew1)) * jnp.einsum('btd,edh->beth', x, ew2)
        eout = jnp.einsum('beth,ehd->betd', h, ew3)
        routed = jnp.einsum('betd,bte->btd', eout, gates)
        return shared + routed
    x = L0_attn_x
    x = _layernorm(x + _L0_attn_ref(x, L0_attn_sink_bias, L0_attn_Wq, L0_attn_bq, L0_attn_Wk, L0_attn_bk, L0_attn_Wv, L0_attn_bv, L0_attn_Wo, L0_attn_bo), axis=-1)
    x = _layernorm(x + _L0_ffn_ref(x, L0_ffn_sw1, L0_ffn_sw2, L0_ffn_sw3, L0_ffn_ew1, L0_ffn_ew2, L0_ffn_ew3, L0_ffn_rw, L0_ffn_rb), axis=-1)
    return x

_drawn_inputs = setup_inputs


def setup_inputs(seed=0):
    import zlib

    import numpy as np

    out = dict(_drawn_inputs(seed))
    spreads = {'L0_attn_bq': (0.0, 0.8),
     'L0_attn_bk': (0.0, 2.0),
     'L0_attn_bv': (0.0, 0.347),
     'L0_attn_bo': (0.0, 0.1)}
    factors = {'L0_attn_Wq': 8.0,
     'L0_attn_Wk': 8.0,
     'L0_attn_Wv': 6.271,
     'L0_ffn_sw1': 6.94,
     'L0_ffn_sw2': 6.906,
     'L0_ffn_sw3': 6.858,
     'L0_ffn_ew1': 8.0,
     'L0_ffn_ew2': 8.0,
     'L0_ffn_ew3': 8.0,
     'L0_ffn_rw': 8.0,
     'L0_ffn_rb': 8.0}
    for name, (base, spread) in spreads.items():
        noise = np.random.default_rng([zlib.crc32(name.encode()), seed]).standard_normal(out[name].shape)
        drawn = base * np.exp(spread * noise) if base else spread * noise
        out[name] = jnp.asarray(drawn.astype(out[name].dtype))
    for name, factor in factors.items():
        out[name] = (out[name] * factor).astype(out[name].dtype)
    return out
```

```python
from contextlib import ExitStack

import concourse.bass as bass
from concourse import mybir

ALU = mybir.AluOpType
ACT = mybir.ActivationFunctionType
AX = mybir.AxisListType
F32 = mybir.dt.float32
F32R = mybir.dt.float32r
BF16 = mybir.dt.bfloat16
U32 = mybir.dt.uint32

P = 128
D = 128
TOKENS = 2048
HEADS, GROUPS, HD = 8, 2, 16
HPG = HEADS // GROUPS
GD = GROUPS * HD
WIN = 32
EXPERTS = 8
FFNS = EXPERTS + 1
HIDDEN = 256
CT = 512
CHUNKS = TOKENS // CT
CHUNKS_PER_SEQUENCE = 2
ROWT = CT // P
QB = 32
BLOCKS = CT // QB
BPG = P // GD
SETS = BLOCKS // BPG
TILES = FFNS * HIDDEN // P
LAG = 2
RING = 3
VW = GD + GROUPS
LN_EPS = 1e-5
SCALE = float(HD) ** -0.5
FP16_MIN = -65504.0
MASKED = -262144.0

C_ID = 0
C_GSEL = C_ID + P
C_QSEL = C_GSEL + EXPERTS * P
C_MASK = C_QSEL + P
C_IOTA = C_MASK + (BPG + 1) * P
C_DEN = C_IOTA + EXPERTS
C_KMASK = C_DEN + GROUPS
C_VMASK = C_KMASK + GROUPS
C_END = C_VMASK + 1

W_Q = 0
W_K = W_Q + P
W_V = W_K + GD
W_O = W_V + P
W_R = W_O + P
W_END = W_R + P

B_Q, B_K, B_V, B_SINK, B_R, B_O = 0, 1, 2, 3, 4, 4 + EXPERTS
B_END = B_O + D

WEIGHT_LOTS = [(0, 1), (1, 3), (3, 6), (6, 9)]

LAST = CHUNKS - 1
SETUP_STEPS = 9


def build(nc, x_cols, x_rows, proj_w, biases, consts, up_w, down_w, out):
    ctx = ExitStack()
    with ctx:
        def sb(name, shape, dt=F32):
            return ctx.enter_context(nc.sbuf_tensor(name, shape, dt))

        def bank(name):
            return ctx.enter_context(nc.psum_tensor(name, [P, CT], F32))

        def sem(name):
            return ctx.enter_context(nc.semaphore(name))

        cst = sb("cst", [P, C_END])
        pw = sb("pw", [P, W_END])
        bias = sb("bias", [P, B_END])
        xT = sb("xT", [P, TOKENS])
        xr = sb("xr", [P, CHUNKS * ROWT, D])
        up_f = sb("up_f", [P, FFNS, 2 * HIDDEN])
        down_f = sb("down_f", [P, FFNS, 2, D])
        up_hi = sb("up_hi", [P, FFNS, 2 * HIDDEN], F32R)
        up_lo = sb("up_lo", [P, FFNS, 2 * HIDDEN], F32R)
        down_hi = sb("down_hi", [P, FFNS, 2, D], F32R)
        down_lo = sb("down_lo", [P, FFNS, 2, D], F32R)
        gsel = sb("gsel", [P, EXPERTS, P], F32R)
        qsel = sb("qsel", [P, P], BF16)
        mask = sb("mask", [P, (BPG + 1) * P], BF16)
        eps = sb("eps", [P, ROWT])
        exponent = sb("exponent", [P, ROWT])
        sink4 = sb("sink4", [P, 1])
        qT = sb("qT", [GD, BLOCKS, HPG, QB])
        kM = sb("kM", [GD, GROUPS, QB + CT])
        vT = sb("vT", [P, QB + CT])
        vbd = sb("vbd", [P, BLOCKS * VW + P])
        mx = sb("mx", [P, SETS, BPG * GROUPS])
        mrow = sb("mrow", [P, SETS, BPG * GROUPS])
        shifted = sb("shifted", [P, SETS, CT])
        prob = shifted
        probT = sb("probT", [P, 2, CT])
        esink = sb("esink", [P, SETS, BPG * GROUPS])
        den = sb("den", [P, SETS, BPG * GROUPS])
        rden = sb("rden", [P, SETS, BPG * GROUPS])
        o = sb("o", [P, CT])
        oT = sb("oT", [P, CT])
        res = sb("res", [P, ROWT, D])
        bn1 = sb("bn1", [P, ROWT, 6])
        mv1 = sb("mv1", [P, ROWT, 2])
        vareps1 = sb("vareps1", [P, ROWT])
        rstd1 = sb("rstd1", [P, ROWT])
        x2 = sb("x2", [P, ROWT, D])
        x2T_new = sb("x2T_new", [P, CT])
        x2T = sb("x2T", [P, 2 * CT])
        x2hi = sb("x2hi", [P, 2 * CT], F32R)
        x2lo = sb("x2lo", [P, 2 * CT], F32R)
        logit = sb("logit", [P, ROWT, EXPERTS])
        top = sb("top", [P, ROWT, 8])
        topi = sb("topi", [P, ROWT, 8], U32)
        topf = sb("topf", [P, ROWT, 2])
        pick = sb("pick", [P, 2, ROWT, EXPERTS])
        picked = sb("picked", [P, ROWT, EXPERTS])
        below = sb("below", [P, ROWT, EXPERTS])
        erout = sb("erout", [P, ROWT, EXPERTS])
        etop = sb("etop", [P, ROWT, EXPERTS])
        esum = sb("esum", [P, ROWT])
        rsum = sb("rsum", [P, ROWT])
        gate = sb("gate", [P, ROWT, EXPERTS])
        gparts = sb("gparts", [P, ROWT, 2 * EXPERTS], F32R)
        gT = sb("gT", [P, 2 * CT], F32R)
        xg = sb("xg", [P, 2, CT])
        xghi = sb("xghi", [P, 2, CT], F32R)
        xglo = sb("xglo", [P, 2, CT], F32R)
        sil = sb("sil", [P, 2, CT])
        h = sb("h", [P, 2, CT])
        hhi = sb("hhi", [P, RING, CT], F32R)
        hlo = sb("hlo", [P, RING, CT], F32R)
        ysum = sb("ysum", [P, CT])
        bn2 = sb("bn2", [P, ROWT, 6])
        mv2 = sb("mv2", [P, ROWT, 2])
        vareps2 = sb("vareps2", [P, ROWT])
        rstd2 = sb("rstd2", [P, ROWT])
        result = sb("result", [P, ROWT, D])

        gate_bank = [bank("gate_bank0"), bank("gate_bank1")]
        up_bank = [bank("up_bank0"), bank("up_bank1")]
        y_bank = bank("y_bank")
        s_bank = bank("s_bank")
        t_bank = bank("t_bank")
        m_bank = bank("m_bank")

        const_in = sem("const_in")
        proj_in = sem("proj_in")
        xcol0_in = sem("xcol0_in")
        xcols_in = sem("xcols_in")
        xrows_in = sem("xrows_in")
        weights_in = [sem(f"weights_in{n}") for n in range(len(WEIGHT_LOTS))]
        setup_done = sem("setup_done")
        weights_hi = sem("weights_hi")
        weights_lo = sem("weights_lo")
        xbias_done = sem("xbias_done")
        exponent_done = sem("exponent_done")
        q_mm, k_mm, v_mm = sem("q_mm"), sem("k_mm"), sem("v_mm")
        q_sb = sem("q_sb")
        k_carried = sem("k_carried")
        k_sb = sem("k_sb")
        v_carried = sem("v_carried")
        v_sb = sem("v_sb")
        vbd_done = sem("vbd_done")
        score_mm = sem("score_mm")
        max_done = sem("max_done")
        mrow_done = sem("mrow_done")
        shift_done = sem("shift_done")
        exp_done = sem("exp_done")
        esink_done = sem("esink_done")
        probT_mm = sem("probT_mm")
        probT_sb = sem("probT_sb")
        pv_mm = sem("pv_mm")
        den_done = sem("den_done")
        rden_done = sem("rden_done")
        o_done = sem("o_done")
        oT_done = sem("oT_done")
        proj_mm = sem("proj_mm")
        res_done = sem("res_done")
        bn1_done = sem("bn1_done")
        mv1_done = sem("mv1_done")
        vareps1_done = sem("vareps1_done")
        rstd1_done = sem("rstd1_done")
        x2_done = sem("x2_done")
        x2T_mm = sem("x2T_mm")
        x2T_sb = sem("x2T_sb")
        x2hi_done = sem("x2hi_done")
        x2lo_done = sem("x2lo_done")
        router_mm = sem("router_mm")
        logit_done = sem("logit_done")
        top_done = sem("top_done")
        topi_done = sem("topi_done")
        topf_done = sem("topf_done")
        below_done = sem("below_done")
        pick_done = sem("pick_done")
        picked_done = sem("picked_done")
        erout_done = sem("erout_done")
        etop_done = sem("etop_done")
        esum_done = sem("esum_done")
        rsum_done = sem("rsum_done")
        gate_done = sem("gate_done")
        ghi_done = sem("ghi_done")
        gparts_done = sem("gparts_done")
        gT_mm = sem("gT_mm")
        gT_sb = sem("gT_sb")
        gcast_mm = sem("gcast_mm")
        xg_done = sem("xg_done")
        xghi_done = sem("xghi_done")
        xglo_done = sem("xglo_done")
        gate_mm = sem("gate_mm")
        up_mm = sem("up_mm")
        silu_done = sem("silu_done")
        h_done = sem("h_done")
        hhi_done = sem("hhi_done")
        hlo_done = sem("hlo_done")
        down_mm = sem("down_mm")
        ysum_done = sem("ysum_done")
        yT_mm = sem("yT_mm")
        bn2_done = sem("bn2_done")
        mv2_done = sem("mv2_done")
        vareps2_done = sem("vareps2_done")
        rstd2_done = sem("rstd2_done")
        result_done = sem("result_done")
        stored = sem("stored")

        def tokens(n):
            return bass.ds(n * CT, CT)

        def slot(n):
            return bass.ds((n % 2) * CT, CT)

        def after(eng, semaphore, count):
            if not (isinstance(count, int) and count <= 0):
                eng.wait_ge(semaphore, count)

        def stand_alone(eng):
            eng.wait_ge(const_in, 32)

        def blocks(ap, width):
            return ap.rearrange("p (b w) -> p b w", w=width)

        sets = [slice(s * BPG * QB, (s + 1) * BPG * QB) for s in range(SETS)]
        block = ctx.enter_context(nc.Block())

        @block.sync
        def _(sp):
            sp.dma_start(pw[:, :], proj_w).then_inc(proj_in, 16)
            sp.dma_start(xT[:, 0:CT], x_cols[:, 0:CT]).then_inc(xcol0_in, 16)
            sp.dma_start(xr[:, :, :], x_rows.rearrange("(t p) d -> p t d", p=P)).then_inc(xrows_in, 16)
            for n, (e0, e1) in enumerate(WEIGHT_LOTS):
                sp.dma_start(up_f[:, e0:e1, :], up_w[:, e0:e1, :]).then_inc(weights_in[n], 16)
                sp.dma_start(down_f[:, e0:e1, :, :], down_w[:, e0:e1, :, :]).then_inc(weights_in[n], 16)
            sp.dma_start(xT[:, CT:TOKENS], x_cols[:, CT:TOKENS]).then_inc(xcols_in, 16)
            with sp.Fori(0, CHUNKS) as c:
                sp.wait_ge(result_done, c + 1)
                sp.dma_start(out[bass.ds(c * CT, CT), :].rearrange("(t p) d -> p t d", p=P),
                             result[:, :, :]).then_inc(stored, 16)
            sp.wait_ge(stored, 16 * CHUNKS)

        @block.tensor
        def _(pe):
            ident = cst[:, C_ID:C_ID + P]

            def project_q(n):
                after(pe, gT_sb, n)
                pe.matmul(t_bank[:, :], pw[:, W_Q:W_Q + P], xT[:, tokens(n)],
                          start=True, stop=True).then_inc(q_mm, 1)

            def project_k(n):
                after(pe, logit_done, n)
                pe.matmul(m_bank[:, :], pw[:, W_K:W_K + P], xT[:, tokens(n)],
                          start=True, stop=True).then_inc(k_mm, 1)

            def project_v(n):
                pe.wait_ge(k_sb, GROUPS * (n + 1))
                pe.matmul(m_bank[:, :], pw[:, W_V:W_V + P], xT[:, tokens(n)],
                          start=True, stop=True).then_inc(v_mm, 1)

            def scores(n, s, gates_before):
                if s == 0:
                    pe.wait_ge(q_sb, HPG * (n + 1))
                    pe.wait_ge(k_sb, GROUPS * (n + 1))
                else:
                    pe.wait_ge(shift_done, SETS * n + s)
                after(pe, xg_done, gates_before)
                if s > 0:
                    mask_at = slice(P, P + CT)
                elif isinstance(n, int):
                    mask_at = slice(0, CT)
                else:
                    mask_at = bass.ds((n % CHUNKS_PER_SEQUENCE) * P, CT)
                pe.matmul(s_bank[:, :], qsel[:, :], mask[:, mask_at], start=True, stop=False,
                          skip_group_check=True)
                for j in range(BPG):
                    at = (s * BPG + j) * QB
                    mm = pe.matmul(s_bank[:, j * P:(j + 1) * P], qT[:, s * BPG + j, :, :],
                                   kM[:, :, at:at + 2 * QB],
                                   start=False, stop=(j == BPG - 1), skip_group_check=True)
                mm.then_inc(score_mm, 1)

            def transpose_prob(n, s):
                pe.wait_ge(exp_done, SETS * n + s + 1)
                if s > 0:
                    pe.wait_ge(probT_sb, SETS * n + s)
                for j in range(BPG):
                    mm = pe.transpose(t_bank[:, j * P:(j + 1) * P], prob[:, s, j * P:(j + 1) * P], ident)
                mm.then_inc(probT_mm, 1)

            def weigh_values(n, s):
                if s == 0:
                    pe.wait_ge(vbd_done, n + 1)
                else:
                    pe.wait_ge(o_done, SETS * n + s)
                pe.wait_ge(probT_sb, SETS * n + s + 1)
                for j in range(BPG):
                    at = (s * BPG + j) * VW
                    mm = pe.matmul(m_bank[:, j * P:(j + 1) * P], probT[:, s % 2, j * P:(j + 1) * P],
                                   vbd[:, at:at + P], start=True, stop=True)
                mm.then_inc(pv_mm, 1)

            def project_out(n):
                pe.wait_ge(oT_done, n + 1)
                for j in range(ROWT):
                    mm = pe.matmul(m_bank[:, j * P:(j + 1) * P], oT[:, j * P:(j + 1) * P],
                                   pw[:, W_O:W_O + D], start=True, stop=True)
                mm.then_inc(proj_mm, 1)

            def transpose_x2(n):
                pe.wait_ge(x2_done, n + 1)
                pe.wait_ge(probT_sb, SETS * (n + 1))
                for j in range(ROWT):
                    mm = pe.transpose(t_bank[:, j * P:(j + 1) * P], x2[:, j, :], ident)
                mm.then_inc(x2T_mm, 1)

            def route(n):
                pe.wait_ge(x2T_sb, 2 * n + 1)
                pe.wait_ge(res_done, n + 1)
                for j in range(ROWT):
                    mm = pe.matmul(m_bank[:, j * P:(j + 1) * P], x2T_new[:, j * P:(j + 1) * P],
                                   pw[:, W_R:W_R + P], start=True, stop=True)
                mm.then_inc(router_mm, 1)

            def transpose_gates(n):
                pe.wait_ge(gparts_done, n + 1)
                pe.wait_ge(x2T_sb, 2 * n + 2)
                for j in range(ROWT):
                    mm = pe.transpose(t_bank[0:2 * EXPERTS, j * P:(j + 1) * P],
                                      gparts[:, j, :].bitcast(F32), ident)
                mm.then_inc(gT_mm, 1)

            def broadcast_gate(c, e, scores_before):
                if e == 0:
                    pe.wait_ge(gT_sb, c + 1)
                    after(pe, result_done, c)
                else:
                    pe.wait_ge(xg_done, EXPERTS * c + e)
                pe.wait_ge(shift_done, scores_before)
                pe.matmul(s_bank[:, :], gsel[:, e, :], gT[:, slot(c)],
                          start=True, stop=True).then_inc(gcast_mm, 1)

            def triple(into, w_hi, w_lo, m_hi, m_lo, start, stop):
                pe.matmul(into, w_hi, m_hi, start=start, stop=False)
                pe.matmul(into, w_lo, m_hi, start=False, stop=False)
                return pe.matmul(into, w_hi, m_lo, start=False, stop=stop)

            def up(c, t):
                f, k = divmod(t, 2)
                if t < 2:
                    pe.wait_ge(x2lo_done, c + 1)
                    pe.wait_ge(x2hi_done, c + 1)
                    after(pe, silu_done, TILES * c)
                else:
                    pe.wait_ge(silu_done, TILES * c + t - 1)
                w1 = slice(k * P, (k + 1) * P)
                w2 = slice(HIDDEN + k * P, HIDDEN + (k + 1) * P)
                triple(gate_bank[t % 2][:, :], up_hi[:, f, w1], up_lo[:, f, w1],
                       x2hi[:, slot(c)], x2lo[:, slot(c)], True, True).then_inc(gate_mm, 1)
                if f == 0:
                    after(pe, h_done, TILES * c)
                    m_hi, m_lo = x2hi[:, slot(c)], x2lo[:, slot(c)]
                else:
                    pe.wait_ge(h_done, TILES * c + t - 1)
                    pe.wait_ge(xglo_done, EXPERTS * c + f)
                    m_hi, m_lo = xghi[:, (f - 1) % 2, :], xglo[:, (f - 1) % 2, :]
                triple(up_bank[t % 2][:, :], up_hi[:, f, w2], up_lo[:, f, w2],
                       m_hi, m_lo, True, True).then_inc(up_mm, 1)

            def down(c, t):
                f, k = divmod(t, 2)
                if t == 0:
                    after(pe, ysum_done, c)
                pe.wait_ge(hlo_done, TILES * c + t + 1)
                triple(y_bank[:, :], down_hi[:, f, k, :], down_lo[:, f, k, :],
                       hhi[:, t % RING, :], hlo[:, t % RING, :],
                       t == 0, t == TILES - 1).then_inc(down_mm, 1)

            def transpose_result(c):
                pe.wait_ge(ysum_done, c + 1)
                pe.wait_ge(xg_done, EXPERTS * (c + 1))
                for j in range(ROWT):
                    mm = pe.transpose(s_bank[:, j * P:(j + 1) * P], ysum[:, j * P:(j + 1) * P], ident)
                mm.then_inc(yT_mm, 1)

            def feed_forward(c, n):
                first_of_lot = {2 * e0: lot for lot, (e0, _) in enumerate(WEIGHT_LOTS)}
                for t in range(TILES + LAG):
                    if t < TILES:
                        if t in first_of_lot:
                            pe.wait_ge(weights_lo, first_of_lot[t] + 1)
                        up(c, t)
                    if t % 2 == 0 and t // 2 < EXPERTS:
                        seen = SETS * (c + 1)
                        if n is not None:
                            seen = SETS * n + min(max(t - 3, 0), SETS)
                        broadcast_gate(c, t // 2, seen)
                    if n is not None:
                        if t == 0:
                            project_q(n)
                        if t == 1:
                            project_k(n)
                        if t == 2:
                            project_v(n)
                        if 3 <= t <= 6:
                            scores(n, t - 3, EXPERTS * c + t // 2 + 1)
                        if 6 <= t <= 9:
                            transpose_prob(n, t - 6)
                        if 7 <= t <= 10:
                            weigh_values(n, t - 7)
                        if t == 12:
                            project_out(n)
                        if t == 14:
                            transpose_x2(n)
                        if t == 15:
                            route(n)
                    if t >= LAG:
                        down(c, t - LAG)
                if n is not None:
                    transpose_gates(n)
                transpose_result(c)

            pe.wait_ge(proj_in, 16)
            pe.wait_ge(xcol0_in, 16)
            project_q(0)
            project_k(0)
            project_v(0)
            pe.wait_ge(setup_done, SETUP_STEPS)
            pe.wait_ge(const_in, 32)
            scores(0, 0, 0)
            for s in range(1, SETS):
                scores(0, s, 0)
                transpose_prob(0, s - 1)
                if s > 1:
                    weigh_values(0, s - 2)
            transpose_prob(0, SETS - 1)
            weigh_values(0, SETS - 2)
            weigh_values(0, SETS - 1)
            project_out(0)
            transpose_x2(0)
            route(0)
            transpose_gates(0)
            pe.wait_ge(xcols_in, 16)
            with pe.Fori(0, LAST) as c:
                feed_forward(c, c + 1)
            feed_forward(LAST, None)

        @block.scalar
        def _(act):
            act.dma_start(cst[:, :], consts).then_inc(const_in, 16)
            act.dma_start(bias[:, :], biases).then_inc(const_in, 16)

            def queries(n):
                act.wait_ge(q_mm, n + 1)
                after(act, score_mm, SETS * n)
                for i in range(HPG):
                    rows = slice(GD * i, GD * (i + 1))
                    act.activation(qT[:, :, i, :], blocks(t_bank[rows, :], QB), ACT.Identity,
                                   bias=bias[rows, B_Q:B_Q + 1]).then_inc(q_sb, 1)

            def exps(n, s):
                act.wait_ge(shift_done, SETS * n + s + 1)
                act.activation(prob[:, s, :], shifted[:, s, :], ACT.Exp, scale=SCALE).then_inc(exp_done, 1)
                act.activation(esink[:, s, :], mrow[:, s, :], ACT.Exp, scale=-SCALE,
                               bias=bias[:, B_SINK:B_SINK + 1]).then_inc(esink_done, 1)

            def prob_out(n, s):
                act.wait_ge(probT_mm, SETS * n + s + 1)
                after(act, pv_mm, SETS * n + max(s - 1, 0))
                act.activation(probT[:, s % 2, :], t_bank[:, :], ACT.Copy).then_inc(probT_sb, 1)

            def x2T_out(n):
                act.wait_ge(x2T_mm, n + 1)
                after(act, x2lo_done, n)
                act.activation(x2T_new[:, :], t_bank[:, :], ACT.Copy).then_inc(x2T_sb, 1)
                act.activation(x2T[:, slot(n)], t_bank[:, :], ACT.Copy).then_inc(x2T_sb, 1)

            def router_exp(n):
                act.wait_ge(below_done, n + 1)
                act.activation(erout[:, :, :], below[:, :, :], ACT.Exp).then_inc(erout_done, 1)

            def gates_out(n):
                act.wait_ge(gT_mm, n + 1)
                act.activation(gT[0:2 * EXPERTS, slot(n)], t_bank[0:2 * EXPERTS, :], ACT.Copy).then_inc(gT_sb, 1)

            def weights_out(lot):
                e0, e1 = WEIGHT_LOTS[lot]
                act.wait_ge(weights_in[lot], 32)
                act.activation(up_hi[:, e0:e1, :], up_f[:, e0:e1, :], ACT.Copy)
                act.activation(down_hi[:, e0:e1, :, :], down_f[:, e0:e1, :, :], ACT.Copy).then_inc(weights_hi, 1)

            def silu(c, t):
                act.wait_ge(gate_mm, TILES * c + t + 1)
                after(act, h_done, TILES * c + max(t - 1, 0))
                act.activation(sil[:, t % 2, :], gate_bank[t % 2][:, :], ACT.Silu).then_inc(silu_done, 1)

            def h_high(c, t):
                act.wait_ge(h_done, TILES * c + t + 1)
                after(act, down_mm, TILES * c + max(t - RING + 1, 0))
                act.activation(hhi[:, t % RING, :], h[:, t % 2, :], ACT.Copy).then_inc(hhi_done, 1)

            def xg_high(c, e):
                act.wait_ge(xg_done, EXPERTS * c + e + 1)
                if e >= 2:
                    act.wait_ge(up_mm, TILES * c + 2 * e)
                else:
                    after(act, up_mm, TILES * c)
                act.activation(xghi[:, e % 2, :], xg[:, e % 2, :], ACT.Copy).then_inc(xghi_done, 1)

            def feed_forward(c, n):
                for t in range(TILES + 1):
                    if t < TILES:
                        silu(c, t)
                    if t > 0:
                        h_high(c, t - 1)
                    if t % 2 == 0 and t // 2 < EXPERTS:
                        xg_high(c, t // 2)
                    if n is not None:
                        if t == 0:
                            queries(n)
                        if t == 5:
                            exps(n, 0)
                            exps(n, 1)
                        if 7 <= t <= 10:
                            prob_out(n, t - 7)
                        if t == 7:
                            exps(n, 2)
                            exps(n, 3)
                        if t == 14:
                            x2T_out(n)
                        if t == 16:
                            router_exp(n)
                if n is not None:
                    gates_out(n)

            act.wait_ge(const_in, 32)
            queries(0)
            exps(0, 0)
            for s in range(1, SETS):
                exps(0, s)
                prob_out(0, s - 1)
            prob_out(0, SETS - 1)
            for lot in range(len(WEIGHT_LOTS)):
                weights_out(lot)
            x2T_out(0)
            router_exp(0)
            gates_out(0)
            with act.Fori(0, LAST) as c:
                feed_forward(c, c + 1)
            feed_forward(LAST, None)

        @block.vector
        def _(dve):
            def keys(n):
                after(dve, score_mm, SETS * n)
                if not isinstance(n, int):
                    dve.tensor_copy(kM[:, :, 0:QB], kM[:, :, CT:CT + QB]).then_inc(k_carried, 1)
                    dve.wait_ge(k_carried, n)
                dve.wait_ge(k_mm, n + 1)
                for g in range(GROUPS):
                    dve.tensor_scalar(kM[:, g, QB:QB + CT], m_bank[0:GD, :], bias[0:GD, B_K:B_K + 1],
                                      cst[0:GD, C_KMASK + g:C_KMASK + g + 1],
                                      ALU.add, ALU.mult).then_inc(k_sb, 1)

            def values(n):
                if not isinstance(n, int):
                    dve.wait_ge(vbd_done, n)
                    for g in range(GROUPS):
                        rows = slice(g * P // 2, g * P // 2 + GD)
                        dve.tensor_copy(vT[rows, 0:QB], vT[rows, CT:CT + QB]).then_inc(v_carried, 1)
                    dve.wait_ge(v_carried, GROUPS * n)
                dve.wait_ge(v_mm, n + 1)
                for quadrant in range(P // GD):
                    rows = slice(quadrant * GD, (quadrant + 1) * GD)
                    at = QB * (1 - quadrant % 2)
                    dve.tensor_scalar(vT[rows, at:at + CT], m_bank[rows, :], bias[rows, B_V:B_V + 1],
                                      cst[rows, C_VMASK:C_VMASK + 1], ALU.add, ALU.mult).then_inc(v_sb, 1)
                dve.wait_ge(v_sb, P // GD * (n + 1))
                after(dve, pv_mm, SETS * n)
                dve.transpose(blocks(vbd[:, 0:BLOCKS * VW], VW)[:, :, 0:GD],
                              blocks(vT[:, 0:CT], QB)).then_inc(vbd_done, 1)

            def softmax_shift(n, s):
                at = SETS * n + s + 1
                by_row = "p (i k) -> p i k"
                dve.wait_ge(score_mm, at)
                dve.tensor_reduce(mx[:, s, :], s_bank[:, :].rearrange(by_row, k=2 * QB),
                                  AX.X, ALU.max).then_inc(max_done, 1)
                dve.wait_ge(max_done, at)
                dve.tensor_scalar(mrow[:, s, :], mx[:, s, :], sink4[:, :], None, ALU.max).then_inc(mrow_done, 1)
                dve.wait_ge(mrow_done, at)
                dve.tensor_tensor(shifted[:, s, :].rearrange(by_row, k=2 * QB),
                                  s_bank[:, :].rearrange(by_row, k=2 * QB),
                                  mrow[:, s, :].unsqueeze(2).to_broadcast([P, BPG * GROUPS, 2 * QB]),
                                  ALU.subtract).then_inc(shift_done, 1)

            def normalise(n, s):
                at = SETS * n + s + 1
                weighed = blocks(m_bank[:, :], P)
                by_group = "p (b g) -> p b g"
                dve.wait_ge(esink_done, at)
                dve.wait_ge(pv_mm, at)
                dve.tensor_tensor(den[:, s, :].rearrange(by_group, b=BPG), weighed[:, :, GD:VW],
                                  esink[:, s, :].rearrange(by_group, b=BPG), ALU.add).then_inc(den_done, 1)
                dve.wait_ge(den_done, at)
                dve.reciprocal(rden[:, s, :], den[:, s, :]).then_inc(rden_done, 1)
                dve.wait_ge(rden_done, at)
                dve.tensor_tensor(o[:, sets[s]].rearrange("p (b g d) -> p b g d", b=BPG, g=GROUPS),
                                  weighed[:, :, 0:GD].rearrange("p b (g d) -> p b g d", g=GROUPS),
                                  rden[:, s, :].rearrange(by_group, b=BPG).unsqueeze(3)
                                  .to_broadcast([P, BPG, GROUPS, HD]), ALU.mult).then_inc(o_done, 1)

            def turn(n):
                dve.wait_ge(o_done, SETS * (n + 1))
                after(dve, proj_mm, n)
                dve.transpose(oT[:, :], o[:, :]).then_inc(oT_done, 1)

            def norm1(n):
                dve.wait_ge(proj_mm, n + 1)
                dve.tensor_tensor(res[:, :, :], blocks(m_bank[:, :], D),
                                  xr[:, bass.ds(n * ROWT, ROWT), :], ALU.add).then_inc(res_done, 1)
                dve.wait_ge(res_done, n + 1)
                for j in range(ROWT):
                    ins = dve.bn_stats(bn1[:, j, :], res[:, j, :])
                ins.then_inc(bn1_done, 1)
                stand_alone(dve)
                dve.wait_ge(bn1_done, n + 1)
                for j in range(ROWT):
                    ins = dve.bn_aggr(mv1[:, j, :], bn1[:, j, :])
                ins.then_inc(mv1_done, 1)

            def scale1(n):
                dve.wait_ge(rstd1_done, n + 1)
                for j in range(ROWT):
                    ins = dve.tensor_scalar(x2[:, j, :], res[:, j, :], mv1[:, j, 0:1], rstd1[:, j:j + 1],
                                            ALU.subtract, ALU.mult)
                ins.then_inc(x2_done, 1)

            def x2_high(n):
                dve.wait_ge(x2T_sb, 2 * n + 1)
                dve.tensor_copy(x2hi[:, slot(n)], x2T_new[:, :]).then_inc(x2hi_done, 1)

            def logits(n):
                every = [P, ROWT, EXPERTS]
                dve.wait_ge(router_mm, n + 1)
                dve.tensor_tensor(logit[:, :, :], blocks(m_bank[:, :], P)[:, :, 0:EXPERTS],
                                  bias[:, B_R:B_R + EXPERTS].unsqueeze(1).to_broadcast(every),
                                  ALU.add).then_inc(logit_done, 1)
                stand_alone(dve)
                dve.wait_ge(logit_done, n + 1)
                for j in range(ROWT):
                    ins = dve.max(top[:, j, :], logit[:, j, :])
                ins.then_inc(top_done, 1)
                dve.wait_ge(top_done, n + 1)
                dve.tensor_tensor(below[:, :, :], logit[:, :, :], top[:, :, 0:1].to_broadcast(every),
                                  ALU.subtract).then_inc(below_done, 1)
                for j in range(ROWT):
                    ins = dve.max_index(topi[:, j, :], top[:, j, :], logit[:, j, :])
                ins.then_inc(topi_done, 1)
                dve.wait_ge(topi_done, n + 1)
                dve.tensor_copy(topf[:, :, :], topi[:, :, 0:2]).then_inc(topf_done, 1)
                dve.wait_ge(topf_done, n + 1)
                for i in range(2):
                    ins = dve.tensor_tensor(pick[:, i, :, :],
                                            cst[:, C_IOTA:C_IOTA + EXPERTS].unsqueeze(1).to_broadcast(every),
                                            topf[:, :, i:i + 1].to_broadcast(every), ALU.is_equal)
                ins.then_inc(pick_done, 1)
                dve.wait_ge(pick_done, n + 1)
                dve.tensor_tensor(picked[:, :, :], pick[:, 0, :, :], pick[:, 1, :, :], ALU.add)\
                   .then_inc(picked_done, 1)

            def gates(n):
                every = [P, ROWT, EXPERTS]
                dve.wait_ge(erout_done, n + 1)
                dve.wait_ge(picked_done, n + 1)
                dve.tensor_tensor(etop[:, :, :], erout[:, :, :], picked[:, :, :], ALU.mult).then_inc(etop_done, 1)
                dve.wait_ge(etop_done, n + 1)
                dve.tensor_reduce(esum[:, :], etop[:, :, :], AX.X, ALU.add).then_inc(esum_done, 1)
                dve.wait_ge(esum_done, n + 1)
                dve.reciprocal(rsum[:, :], esum[:, :]).then_inc(rsum_done, 1)
                dve.wait_ge(rsum_done, n + 1)
                dve.tensor_tensor(gate[:, :, :], etop[:, :, :], rsum[:, :].unsqueeze(2).to_broadcast(every),
                                  ALU.mult).then_inc(gate_done, 1)
                dve.wait_ge(gate_done, n + 1)
                dve.tensor_copy(gparts[:, :, 0:EXPERTS], gate[:, :, :]).then_inc(ghi_done, 1)
                dve.wait_ge(ghi_done, n + 1)
                dve.tensor_tensor(gparts[:, :, EXPERTS:2 * EXPERTS], gate[:, :, :],
                                  gparts[:, :, 0:EXPERTS].bitcast(F32), ALU.subtract).then_inc(gparts_done, 1)

            def gated_input(c, e):
                dve.wait_ge(gcast_mm, EXPERTS * c + e + 1)
                after(dve, xglo_done, EXPERTS * c + max(e - 1, 0))
                dve.tensor_tensor(xg[:, e % 2, :], x2T[:, slot(c)], s_bank[:, :], ALU.mult)\
                   .then_inc(xg_done, 1)

            def hidden(c, t):
                dve.wait_ge(silu_done, TILES * c + t + 1)
                dve.wait_ge(up_mm, TILES * c + t + 1)
                after(dve, hlo_done, TILES * c + max(t - 1, 0))
                dve.tensor_tensor(h[:, t % 2, :], sil[:, t % 2, :], up_bank[t % 2][:, :], ALU.mult)\
                   .then_inc(h_done, 1)

            def sum_y(c):
                dve.wait_ge(down_mm, TILES * (c + 1))
                after(dve, yT_mm, c)
                dve.tensor_tensor(ysum[:, :], x2T[:, slot(c)], y_bank[:, :], ALU.add).then_inc(ysum_done, 1)

            def norm2(c):
                dve.wait_ge(yT_mm, c + 1)
                for j in range(ROWT):
                    ins = dve.bn_stats(bn2[:, j, :], s_bank[:, j * D:(j + 1) * D])
                ins.then_inc(bn2_done, 1)
                stand_alone(dve)
                dve.wait_ge(bn2_done, c + 1)
                for j in range(ROWT):
                    ins = dve.bn_aggr(mv2[:, j, :], bn2[:, j, :])
                ins.then_inc(mv2_done, 1)
                dve.wait_ge(rstd2_done, c + 1)
                after(dve, stored, 16 * c)
                for j in range(ROWT):
                    ins = dve.tensor_scalar(result[:, j, :], s_bank[:, j * D:(j + 1) * D],
                                            mv2[:, j, 0:1], rstd2[:, j:j + 1], ALU.subtract, ALU.mult)
                ins.then_inc(result_done, 1)

            def weights_low(lot):
                e0, e1 = WEIGHT_LOTS[lot]
                dve.wait_ge(weights_hi, lot + 1)
                dve.tensor_tensor(up_lo[:, e0:e1, :], up_f[:, e0:e1, :], up_hi[:, e0:e1, :].bitcast(F32),
                                  ALU.subtract)
                dve.tensor_tensor(down_lo[:, e0:e1, :, :], down_f[:, e0:e1, :, :],
                                  down_hi[:, e0:e1, :, :].bitcast(F32), ALU.subtract).then_inc(weights_lo, 1)

            def feed_forward(c, n):
                for t in range(TILES):
                    if t % 2 == 0 and t // 2 < EXPERTS:
                        gated_input(c, t // 2)
                    hidden(c, t)
                    if n is not None:
                        if t == 1:
                            keys(n)
                        if t == 2:
                            values(n)
                        if 3 <= t <= 6:
                            softmax_shift(n, t - 3)
                        if 7 <= t <= 10:
                            normalise(n, t - 7)
                        if t == 11:
                            turn(n)
                        if t == 12:
                            norm1(n)
                        if t == 13:
                            scale1(n)
                        if t == 14:
                            x2_high(n)
                        if t == 15:
                            logits(n)
                        if t == 16:
                            gates(n)
                sum_y(c)
                norm2(c)

            dve.memset(vbd[:, :], 0.0).then_inc(setup_done, 1)
            dve.memset(kM[:, :, 0:QB], 0.0).then_inc(setup_done, 1)
            dve.memset(vT[:, :], 0.0).then_inc(setup_done, 1)
            dve.memset(gT[:, :].bitcast(F32), 0.0).then_inc(setup_done, 1)
            dve.wait_ge(const_in, 32)
            dve.tensor_copy(qsel[:, :], cst[:, C_QSEL:C_QSEL + P]).then_inc(setup_done, 1)
            dve.tensor_copy(mask[:, :], cst[:, C_MASK:C_MASK + (BPG + 1) * P]).then_inc(setup_done, 1)
            dve.tensor_scalar(sink4[:, :], bias[:, B_SINK:B_SINK + 1], FP16_MIN, 1.0 / SCALE,
                              ALU.max, ALU.mult).then_inc(setup_done, 1)
            dve.wait_ge(setup_done, 3)
            dve.tensor_copy(blocks(vbd[:, 0:BLOCKS * VW], VW)[:, :, GD:VW],
                            cst[:, C_DEN:C_DEN + GROUPS].unsqueeze(1).to_broadcast([P, BLOCKS, GROUPS]))\
               .then_inc(setup_done, 1)
            dve.tensor_copy(gsel[:, :, :], cst[:, C_GSEL:C_GSEL + EXPERTS * P]
                            .rearrange("p (e q) -> p e q", e=EXPERTS)).then_inc(setup_done, 1)
            keys(0)
            values(0)
            dve.wait_ge(setup_done, SETUP_STEPS)
            softmax_shift(0, 0)
            for s in range(1, SETS):
                softmax_shift(0, s)
                if s > 1:
                    normalise(0, s - 2)
            normalise(0, SETS - 2)
            normalise(0, SETS - 1)
            turn(0)
            dve.wait_ge(xbias_done, 1)
            norm1(0)
            scale1(0)
            x2_high(0)
            logits(0)
            gates(0)
            for lot in range(len(WEIGHT_LOTS)):
                weights_low(lot)
            with dve.Fori(0, LAST) as c:
                feed_forward(c, c + 1)
            feed_forward(LAST, None)

        @block.gpsimd
        def _(pool):
            def rstd(mv, vareps, into, ready, added, done, n):
                pool.wait_ge(ready, n + 1)
                pool.tensor_tensor(vareps[:, :], mv[:, :, 1], eps[:, :], ALU.add).then_inc(added, 1)
                pool.wait_ge(added, n + 1)
                pool.tensor_tensor(into[:, :], vareps[:, :], exponent[:, :], ALU.pow).then_inc(done, 1)

            def x2_low(n):
                pool.wait_ge(x2hi_done, n + 1)
                pool.tensor_tensor(x2lo[:, slot(n)], x2T_new[:, :], x2hi[:, slot(n)].bitcast(F32),
                                   ALU.subtract).then_inc(x2lo_done, 1)

            def h_low(c, t):
                pool.wait_ge(hhi_done, TILES * c + t + 1)
                pool.tensor_tensor(hlo[:, t % RING, :], h[:, t % 2, :], hhi[:, t % RING, :].bitcast(F32),
                                   ALU.subtract).then_inc(hlo_done, 1)

            def xg_low(c, e):
                pool.wait_ge(xghi_done, EXPERTS * c + e + 1)
                pool.tensor_tensor(xglo[:, e % 2, :], xg[:, e % 2, :], xghi[:, e % 2, :].bitcast(F32),
                                   ALU.subtract).then_inc(xglo_done, 1)

            def feed_forward(c, n):
                for t in range(TILES + 1):
                    if t > 0:
                        h_low(c, t - 1)
                    if t % 2 == 0 and t // 2 < EXPERTS:
                        xg_low(c, t // 2)
                    if n is not None:
                        if t == 13:
                            rstd(mv1, vareps1, rstd1, mv1_done, vareps1_done, rstd1_done, n)
                        if t == 15:
                            x2_low(n)
                rstd(mv2, vareps2, rstd2, mv2_done, vareps2_done, rstd2_done, c)

            pool.memset(eps[:, :], LN_EPS).then_inc(exponent_done, 1)
            pool.memset(exponent[:, :], -0.5).then_inc(exponent_done, 1)
            pool.wait_ge(const_in, 32)
            pool.wait_ge(xrows_in, 16)
            pool.tensor_tensor(xr[:, :, :], xr[:, :, :],
                               bias[:, B_O:B_O + D].unsqueeze(1).to_broadcast([P, CHUNKS * ROWT, D]),
                               ALU.add).then_inc(xbias_done, 1)
            pool.wait_ge(exponent_done, 2)
            rstd(mv1, vareps1, rstd1, mv1_done, vareps1_done, rstd1_done, 0)
            x2_low(0)
            with pool.Fori(0, LAST) as c:
                feed_forward(c, c + 1)
            feed_forward(LAST, None)


def kernel(L0_attn_x, L0_attn_sink_bias, L0_attn_Wq, L0_attn_bq, L0_attn_Wk, L0_attn_bk, L0_attn_Wv,
           L0_attn_bv, L0_attn_Wo, L0_attn_bo, L0_ffn_sw1, L0_ffn_sw2, L0_ffn_sw3, L0_ffn_ew1,
           L0_ffn_ew2, L0_ffn_ew3, L0_ffn_rw, L0_ffn_rb):
    import numpy as np
    import concourse.bacc as bacc
    from concourse.bass_utils import run_bass_kernel_spmd

    def arr(a):
        return np.asarray(a)

    x = arr(L0_attn_x).reshape(TOKENS, D)

    def rows_by_head(a):
        a = arr(a)
        return a.reshape(GROUPS, HPG, HD, *a.shape[1:]).swapaxes(0, 1).reshape(a.shape)

    router = np.zeros((D, P), np.float32)
    router[:, 0:EXPERTS] = arr(L0_ffn_rw)
    proj = np.concatenate([rows_by_head(L0_attn_Wq).T, arr(L0_attn_Wk).T,
                           np.tile(arr(L0_attn_Wv).T, (1, P // GD)),
                           rows_by_head(arr(L0_attn_Wo).T), router], axis=1)

    bias = np.zeros((P, B_END), np.float32)
    bias[:, B_Q] = rows_by_head(L0_attn_bq)
    bias[0:GD, B_K] = arr(L0_attn_bk)
    bias[:, B_V] = np.tile(arr(L0_attn_bv), P // GD)
    bias[:, B_SINK] = arr(L0_attn_sink_bias)
    bias[:, B_R:B_R + EXPERTS] = arr(L0_ffn_rb)
    bias[:, B_O:B_O + D] = arr(L0_attn_bo)

    up = np.concatenate([np.concatenate([arr(L0_ffn_sw1)[None], arr(L0_ffn_ew1)]),
                         np.concatenate([arr(L0_ffn_sw2)[None], arr(L0_ffn_ew2)])], axis=2)
    up = up.transpose(1, 0, 2)
    down = np.concatenate([arr(L0_ffn_sw3)[None], arr(L0_ffn_ew3)])
    down = down.reshape(FFNS, 2, P, D).transpose(2, 0, 1, 3)

    c = np.zeros((P, C_END), np.float32)
    c[:, C_ID:C_ID + P] = np.eye(P)
    for e in range(EXPERTS):
        c[[e, EXPERTS + e], C_GSEL + e * P:C_GSEL + (e + 1) * P] = 1.0
    c[0:QB, C_QSEL:C_QSEL + P] = np.tile(np.eye(QB), (1, HPG))
    q, k = np.arange(QB)[:, None], np.arange(QB)[None, :]
    before = np.where(k > q, 0.0, MASKED)
    own = np.where(k <= q, 0.0, MASKED)
    rest = np.concatenate([before, own] * GROUPS, axis=1)
    first = np.concatenate([np.full((QB, QB), MASKED), own] * GROUPS, axis=1)
    c[0:QB, C_MASK:C_MASK + (BPG + 1) * P] = np.concatenate([first] + [rest] * BPG, axis=1)
    c[:, C_IOTA:C_IOTA + EXPERTS] = np.arange(EXPERTS)
    row = np.arange(P)
    for g in range(GROUPS):
        c[:, C_DEN + g] = row // (2 * QB) == g
        c[0:GD, C_KMASK + g] = row[0:GD] // HD == g
    c[:, C_VMASK] = row // (2 * GD) == (row % GD) // HD

    feeds = {"x_cols": x.T, "x_rows": x, "proj_w": proj, "biases": bias, "consts": c,
             "up_w": up, "down_w": down}
    feeds = {name: np.ascontiguousarray(a) for name, a in feeds.items()}
    nc = bacc.Bacc("TRN2", target_bir_lowering=False, num_devices=1)
    args = [nc.dram_tensor(name, a.shape, mybir.dt.from_np(a.dtype), kind="ExternalInput").ap()
            for name, a in feeds.items()]
    result = nc.dram_tensor("out", (TOKENS, D), F32, kind="ExternalOutput").ap()
    build(nc, *args, result)
    run = run_bass_kernel_spmd(nc, [feeds], core_ids=[0])
    return run.results[0]["out"].reshape(arr(L0_attn_x).shape)
```

```python
from contextlib import ExitStack

import concourse.bass as bass
from concourse import mybir

ALU = mybir.AluOpType
ACT = mybir.ActivationFunctionType
AX = mybir.AxisListType
F32 = mybir.dt.float32
F32R = mybir.dt.float32r
BF16 = mybir.dt.bfloat16
U32 = mybir.dt.uint32

P = 128
D = 128
TOKENS = 2048
HEADS, GROUPS, HD = 8, 2, 16
HPG = HEADS // GROUPS
GD = GROUPS * HD
WIN = 32
EXPERTS = 8
FFNS = EXPERTS + 1
HIDDEN = 256
CT = 512
CHUNKS = TOKENS // CT
CHUNKS_PER_SEQUENCE = 2
ROWT = CT // P
QB = 32
BLOCKS = CT // QB
BPG = P // GD
SETS = BLOCKS // BPG
TILES = FFNS * HIDDEN // P
LAG = 3
RING = 4
VW = GD + GROUPS
LN_EPS = 1e-5
SCALE = float(HD) ** -0.5
FP16_MIN = -65504.0
MASKED = -262144.0

C_ID = 0
C_IOTA = C_ID + P
C_DEN = C_IOTA + EXPERTS
C_GROUP = C_DEN + GROUPS
C_END = C_GROUP + GROUPS

W_Q = 0
W_KV = W_Q + P
W_QKV = W_KV + 2 * GD
W_O = W_QKV
W_R = W_O + P
W_END = W_R + P

B_Q, B_KV, B_SINK, B_R, B_O = 0, 1, 2, 3, 3 + EXPERTS
B_END = B_O + D

WEIGHT_LOTS = [(0, 1), (1, 3), (3, 6), (6, 9)]
FIRST_OF_LOT = {2 * e0: lot for lot, (e0, _) in enumerate(WEIGHT_LOTS)}

KV_AT = (0, 0)
Q_AT = (0, 1)
VBD_AT = (1, 1)
SCORE_AT = [(2, 0), (3, 0), (4, 2), (6, 0)]
EXP_AT = (7, 0)
PROB_AT = [(8, 2), (9, 1), (10, 0), (10, 2)]
VALUE_AT = [(9, 1), (10, 0), (10, 2), (11, 1)]
PROJECT_AT = (12, 1)
SCALE_AT = (14, 0)
X2T_AT = (14, 0)
ROUTE_AT = (14, 2)
WEIGHT_AT = (16, 0)
GATES_AT = (17, 0)
GATED_AT = [(0, 1)] + [(2 * e - 1, 1) for e in range(1, EXPERTS)]
GATED_HIGH_AT = [(t + 1, 0) for t, _ in GATED_AT]
RESULT_AT = (3, 1)
STORE_AT = (5, 0)
SPLIT_AT = [(1, 1), (3, 1)]
SPLIT_LOW_AT = [(2, 1), (5, 1)]

SETUP_STEPS = 7


def build(nc, x_cols, x_rows, proj_w, biases, consts, masks, selectors, up_w, down_w, out):
    ctx = ExitStack()
    with ctx:
        def sb(name, shape, dt=F32):
            return ctx.enter_context(nc.sbuf_tensor(name, shape, dt))

        def bank(name):
            return ctx.enter_context(nc.psum_tensor(name, [P, CT], F32))

        def sem(name):
            return ctx.enter_context(nc.semaphore(name))

        cst = sb("cst", [P, C_END])
        pw = sb("pw", [P, W_END])
        bias = sb("bias", [P, B_END])
        xT = sb("xT", [P, TOKENS])
        xr = sb("xr", [P, CHUNKS * ROWT, D])
        up_f = sb("up_f", [P, FFNS, 2 * HIDDEN])
        down_f = sb("down_f", [P, FFNS, 2, D])
        up_hi = sb("up_hi", [P, FFNS, 2 * HIDDEN], F32R)
        up_lo = sb("up_lo", [P, FFNS, 2 * HIDDEN], F32R)
        down_hi = sb("down_hi", [P, FFNS, 2, D], F32R)
        down_lo = sb("down_lo", [P, FFNS, 2, D], F32R)
        gsel = sb("gsel", [2 * EXPERTS, EXPERTS * P], F32R)
        mask_f = sb("mask_f", [QB, (BPG + 2) * P])
        mask = sb("mask", [QB, (BPG + 2) * P], BF16)
        eps = sb("eps", [P, ROWT])
        exponent = sb("exponent", [P, ROWT])
        sink4 = sb("sink4", [P, 1])
        warm = sb("warm", [P, ROWT])
        qT = sb("qT", [GD, BLOCKS, HPG, QB])
        kM = sb("kM", [GD, GROUPS, QB + CT])
        vT = sb("vT", [P, QB + CT])
        vbd = sb("vbd", [P, BLOCKS * VW + P])
        mx = sb("mx", [P, SETS, BPG * GROUPS])
        mrow = sb("mrow", [P, SETS, BPG * GROUPS])
        shifted = sb("shifted", [P, SETS, CT])
        prob = shifted
        probT = sb("probT", [P, 2, CT])
        esink = sb("esink", [P, SETS, BPG * GROUPS])
        den = sb("den", [P, SETS, BPG * GROUPS])
        rden = sb("rden", [P, SETS, BPG * GROUPS])
        o = sb("o", [P, CT])
        oT = sb("oT", [P, CT])
        res = sb("res", [P, ROWT, D])
        bn1 = sb("bn1", [P, ROWT, 6])
        mv1 = sb("mv1", [P, ROWT, 2])
        vareps1 = sb("vareps1", [P, ROWT])
        rstd1 = sb("rstd1", [P, ROWT])
        x2 = sb("x2", [P, ROWT, D])
        x2T = sb("x2T", [P, 2 * CT])
        x2hi = sb("x2hi", [P, 2 * CT], F32R)
        x2lo = sb("x2lo", [P, 2 * CT], F32R)
        logit = sb("logit", [P, ROWT, EXPERTS])
        top = sb("top", [P, ROWT, 8])
        topi = sb("topi", [P, ROWT, 8], U32)
        topf = sb("topf", [P, ROWT, 2])
        pick = sb("pick", [P, 2, ROWT, EXPERTS])
        picked = sb("picked", [P, ROWT, EXPERTS])
        signed = sb("signed", [P, ROWT, EXPERTS])
        lead = sb("lead", [P, ROWT])
        half = sb("half", [P, ROWT])
        swing = sb("swing", [P, ROWT, EXPERTS])
        gate = sb("gate", [P, ROWT, EXPERTS])
        gparts = sb("gparts", [P, ROWT, 2 * EXPERTS], F32R)
        gT = sb("gT", [2 * EXPERTS, 2 * CT], F32R)
        xg = sb("xg", [P, 2 * CT])
        gsel_f = xg[0:2 * EXPERTS, 0:EXPERTS * P]
        xghi = sb("xghi", [P, 2, CT], F32R)
        xglo = sb("xglo", [P, 2, CT], F32R)
        sil = sb("sil", [P, 2, CT])
        h = sb("h", [P, 2, CT])
        hhi = sb("hhi", [P, RING, CT], F32R)
        hlo = sb("hlo", [P, RING, CT], F32R)
        ysum = sb("ysum", [P, CT])
        bn2 = sb("bn2", [P, ROWT, 6])
        mv2 = sb("mv2", [P, ROWT, 2])
        vareps2 = sb("vareps2", [P, ROWT])
        rstd2 = sb("rstd2", [P, ROWT])
        result = sb("result", [P, ROWT, D])

        gate_bank = [bank("gate_bank0"), bank("gate_bank1")]
        up_bank = [bank("up_bank0"), bank("up_bank1")]
        y_bank = bank("y_bank")
        s_bank = bank("s_bank")
        t_bank = bank("t_bank")
        m_bank = bank("m_bank")

        def score_bank(n, s):
            return m_bank if n > 0 else [s_bank, gate_bank[0], gate_bank[1], y_bank][s]

        def prob_bank(n, s):
            return t_bank if n > 0 else [t_bank, up_bank[0]][s % 2]

        def value_bank(n, s):
            return m_bank if n > 0 else [m_bank, up_bank[1]][s % 2]

        def project_bank(n, j):
            return m_bank if n > 0 else score_bank(n, j)

        const_in = sem("const_in")
        mask_in = sem("mask_in")
        gsel_in = sem("gsel_in")
        qkv_in = sem("qkv_in")
        proj_in = sem("proj_in")
        xcol0_in = sem("xcol0_in")
        xcols_in = sem("xcols_in")
        xrow0_in = sem("xrow0_in")
        xrows_in = sem("xrows_in")
        weights_in = [sem(f"weights_in{n}") for n in range(len(WEIGHT_LOTS))]
        setup_done = sem("setup_done")
        weights_hi = sem("weights_hi")
        weights_lo = sem("weights_lo")
        xbias_done = sem("xbias_done")
        exponent_done = sem("exponent_done")
        q_mm, kv_mm = sem("q_mm"), sem("kv_mm")
        q_sb = sem("q_sb")
        k_carried = sem("k_carried")
        k_sb = sem("k_sb")
        v_carried = sem("v_carried")
        v_sb = sem("v_sb")
        own_v_sb = sem("own_v_sb")
        vbd_done = sem("vbd_done")
        score_mm = sem("score_mm")
        max_done = sem("max_done")
        mrow_done = sem("mrow_done")
        shift_done = sem("shift_done")
        exp_done = sem("exp_done")
        esink_done = sem("esink_done")
        probT_mm = sem("probT_mm")
        probT_sb = sem("probT_sb")
        pv_mm = sem("pv_mm")
        den_done = sem("den_done")
        rden_done = sem("rden_done")
        o_done = sem("o_done")
        oT_done = sem("oT_done")
        proj_mm = sem("proj_mm")
        res_done = sem("res_done")
        bn1_done = sem("bn1_done")
        mv1_done = sem("mv1_done")
        vareps1_done = sem("vareps1_done")
        rstd1_done = sem("rstd1_done")
        x2_done = sem("x2_done")
        x2T_mm = sem("x2T_mm")
        x2T_sb = sem("x2T_sb")
        x2hi_done = sem("x2hi_done")
        x2lo_done = sem("x2lo_done")
        router_mm = sem("router_mm")
        logit_done = sem("logit_done")
        top_done = sem("top_done")
        topi_done = sem("topi_done")
        topf_done = sem("topf_done")
        pick_done = sem("pick_done")
        picked_done = sem("picked_done")
        lead_done = sem("lead_done")
        half_done = sem("half_done")
        halved_done = sem("halved_done")
        swing_done = sem("swing_done")
        gate_done = sem("gate_done")
        ghi_done = sem("ghi_done")
        gparts_done = sem("gparts_done")
        gT_mm = sem("gT_mm")
        gT_sb = sem("gT_sb")
        gcast_mm = sem("gcast_mm")
        xg_done = sem("xg_done")
        xghi_done = sem("xghi_done")
        xglo_done = sem("xglo_done")
        gate_mm = sem("gate_mm")
        up_mm = sem("up_mm")
        silu_done = sem("silu_done")
        h_done = sem("h_done")
        hhi_done = sem("hhi_done")
        hlo_done = sem("hlo_done")
        down_mm = sem("down_mm")
        ysum_done = sem("ysum_done")
        yT_mm = sem("yT_mm")
        bn2_done = sem("bn2_done")
        mv2_done = sem("mv2_done")
        vareps2_done = sem("vareps2_done")
        rstd2_done = sem("rstd2_done")
        result_done = sem("result_done")
        stored = sem("stored")

        def tokens(n):
            return slice(n * CT, (n + 1) * CT)

        def slot(n):
            return slice((n % 2) * CT, (n % 2 + 1) * CT)

        def after(eng, semaphore, count):
            if count > 0:
                eng.wait_ge(semaphore, count)

        def blocks(ap, width):
            return ap.rearrange("p (b w) -> p b w", w=width)

        sets = [slice(s * BPG * QB, (s + 1) * BPG * QB) for s in range(SETS)]
        block = ctx.enter_context(nc.Block())

        @block.sync
        def _(sp):
            rows = x_rows.rearrange("(t p) d -> p t d", p=P)
            sp.dma_start(pw[:, 0:W_QKV], proj_w[:, 0:W_QKV]).then_inc(qkv_in, 16)
            sp.dma_start(xT[:, 0:CT], x_cols[:, 0:CT]).then_inc(xcol0_in, 16)
            sp.dma_start(pw[:, W_QKV:W_END], proj_w[:, W_QKV:W_END]).then_inc(proj_in, 16)
            sp.dma_start(xr[:, 0:ROWT, :], rows[:, 0:ROWT, :]).then_inc(xrow0_in, 16)
            for n, (e0, e1) in enumerate(WEIGHT_LOTS):
                sp.dma_start(up_f[:, e0:e1, :], up_w[:, e0:e1, :]).then_inc(weights_in[n], 16)
                sp.dma_start(down_f[:, e0:e1, :, :], down_w[:, e0:e1, :, :]).then_inc(weights_in[n], 16)
            sp.dma_start(xT[:, CT:TOKENS], x_cols[:, CT:TOKENS]).then_inc(xcols_in, 16)
            sp.dma_start(xr[:, ROWT:, :], rows[:, ROWT:, :]).then_inc(xrows_in, 16)
            for c in range(CHUNKS):
                sp.wait_ge(result_done, c + 1)
                sp.dma_start(out[tokens(c), :].rearrange("(t p) d -> p t d", p=P),
                             result[:, :, :]).then_inc(stored, 16)
            sp.wait_ge(stored, 16 * CHUNKS)

        @block.tensor
        def _(pe):
            ident = cst[:, C_ID:C_ID + P]

            def project_q(n):
                after(pe, gT_sb, n)
                pe.matmul(t_bank[:, :], pw[:, W_Q:W_Q + P], xT[:, tokens(n)],
                          start=True, stop=True).then_inc(q_mm, 1)

            def project_kv(n):
                after(pe, logit_done, n)
                pe.matmul(m_bank[0:2 * GD, :], pw[:, W_KV:W_KV + 2 * GD], xT[:, tokens(n)],
                          start=True, stop=True).then_inc(kv_mm, 1)

            def scores(n, s):
                if s == 0:
                    pe.wait_ge(q_sb, HPG * (n + 1))
                    pe.wait_ge(k_sb, GROUPS * (n + 1))
                if n > 0:
                    pe.wait_ge(v_sb, GROUPS * (n + 1))
                    pe.wait_ge(shift_done, SETS * n + s)
                bank = score_bank(n, s)
                at = P if s == 0 and n % CHUNKS_PER_SEQUENCE == 0 else 2 * P
                pe.matmul(bank[:, :], mask[:, 0:P], mask[:, at:at + CT], start=True, stop=False,
                          skip_group_check=True)
                for j in range(BPG):
                    at = (s * BPG + j) * QB
                    mm = pe.matmul(bank[:, j * P:(j + 1) * P], qT[:, s * BPG + j, :, :],
                                   kM[:, :, at:at + 2 * QB],
                                   start=False, stop=(j == BPG - 1), skip_group_check=True)
                mm.then_inc(score_mm, 1)

            def transpose_prob(n, s):
                pe.wait_ge(exp_done, SETS * n + s + 1)
                if n > 0:
                    pe.wait_ge(q_sb, HPG * (n + 1))
                    after(pe, result_done, n - 1)
                    pe.wait_ge(probT_sb, SETS * n + s)
                else:
                    after(pe, probT_sb, s - 1)
                for j in range(BPG):
                    mm = pe.transpose(prob_bank(n, s)[:, j * P:(j + 1) * P],
                                      prob[:, s, j * P:(j + 1) * P], ident)
                mm.then_inc(probT_mm, 1)

            def weigh_values(n, s):
                if s == 0:
                    pe.wait_ge(vbd_done, n + 1)
                    if n > 0:
                        pe.wait_ge(shift_done, SETS * (n + 1))
                elif n > 0:
                    pe.wait_ge(o_done, SETS * n + s)
                else:
                    after(pe, o_done, s - 1)
                pe.wait_ge(probT_sb, SETS * n + s + 1)
                for j in range(BPG):
                    at = (s * BPG + j) * VW
                    mm = pe.matmul(value_bank(n, s)[:, j * P:(j + 1) * P],
                                   probT[:, s % 2, j * P:(j + 1) * P],
                                   vbd[:, at:at + P], start=True, stop=True)
                mm.then_inc(pv_mm, 1)

            def project_out(n, tiles):
                pe.wait_ge(oT_done, ROWT * n + tiles[-1] + 1)
                for j in tiles:
                    pe.matmul(project_bank(n, j)[:, j * P:(j + 1) * P], oT[:, j * P:(j + 1) * P],
                              pw[:, W_O:W_O + D], start=True, stop=True).then_inc(proj_mm, 1)

            def transpose_x2(n, tiles):
                pe.wait_ge(probT_sb, SETS * (n + 1))
                pe.wait_ge(x2_done, ROWT * n + tiles[-1] + 1)
                for j in tiles:
                    pe.transpose(t_bank[:, j * P:(j + 1) * P], x2[:, j, :], ident).then_inc(x2T_mm, 1)

            def route(n):
                pe.wait_ge(x2T_sb, n + 1)
                pe.wait_ge(res_done, ROWT * (n + 1))
                for j in range(ROWT):
                    mm = pe.matmul(m_bank[:, j * P:(j + 1) * P], x2T[:, (n % 2) * CT + j * P:(n % 2) * CT + (j + 1) * P],
                                   pw[:, W_R:W_R + P], start=True, stop=True)
                mm.then_inc(router_mm, 1)

            def transpose_gates(n):
                pe.wait_ge(gparts_done, n + 1)
                pe.wait_ge(x2T_sb, n + 1)
                for j in range(ROWT):
                    mm = pe.transpose(t_bank[0:2 * EXPERTS, j * P:(j + 1) * P],
                                      gparts[:, j, :].bitcast(F32), ident)
                mm.then_inc(gT_mm, 1)

            def broadcast_gate(c, e):
                if e == 0:
                    pe.wait_ge(gT_sb, c + 1)
                after(pe, xg_done, EXPERTS * c + e)
                pe.matmul(s_bank[:, :], gsel[:, e * P:(e + 1) * P], gT[:, slot(c)],
                          start=True, stop=True).then_inc(gcast_mm, 1)

            def triple(into, w_hi, w_lo, m_hi, m_lo, start, stop):
                pe.matmul(into, w_hi, m_hi, start=start, stop=False)
                pe.matmul(into, w_lo, m_hi, start=False, stop=False)
                return pe.matmul(into, w_hi, m_lo, start=False, stop=stop)

            def first_up(c, t):
                f, k = divmod(t, 2)
                if t == 0:
                    pe.wait_ge(x2hi_done, c + 1)
                    pe.wait_ge(x2lo_done, c + 1)
                if c == 0 and t in FIRST_OF_LOT:
                    pe.wait_ge(weights_lo, FIRST_OF_LOT[t] + 1)
                after(pe, silu_done, TILES * c + t - 1)
                w1 = slice(k * P, (k + 1) * P)
                triple(gate_bank[t % 2][:, :], up_hi[:, f, w1], up_lo[:, f, w1],
                       x2hi[:, slot(c)], x2lo[:, slot(c)], True, True).then_inc(gate_mm, 1)

            def second_up(c, t):
                f, k = divmod(t, 2)
                w2 = slice(HIDDEN + k * P, HIDDEN + (k + 1) * P)
                after(pe, h_done, TILES * c + t - 1)
                if f == 0:
                    m_hi, m_lo = x2hi[:, slot(c)], x2lo[:, slot(c)]
                else:
                    pe.wait_ge(xglo_done, EXPERTS * c + f)
                    m_hi, m_lo = xghi[:, (f - 1) % 2, :], xglo[:, (f - 1) % 2, :]
                triple(up_bank[t % 2][:, :], up_hi[:, f, w2], up_lo[:, f, w2],
                       m_hi, m_lo, True, True).then_inc(up_mm, 1)

            def down(c, t):
                f, k = divmod(t, 2)
                if t == 0:
                    after(pe, ysum_done, c)
                at = TILES * c + t
                pe.wait_ge(hlo_done, at + 1)
                triple(y_bank[:, :], down_hi[:, f, k, :], down_lo[:, f, k, :],
                       hhi[:, at % RING, :], hlo[:, at % RING, :],
                       t == 0, t == TILES - 1).then_inc(down_mm, 1)

            def transpose_result(c):
                pe.wait_ge(ysum_done, c + 1)
                pe.wait_ge(q_sb, HPG * min(c + 3, CHUNKS))
                pe.wait_ge(gT_sb, min(c + 2, CHUNKS))
                for j in range(ROWT):
                    mm = pe.transpose(t_bank[:, j * P:(j + 1) * P], ysum[:, j * P:(j + 1) * P], ident)
                mm.then_inc(yT_mm, 1)

            def beside(c, place):
                n = c + 1
                if place == RESULT_AT and c > 0:
                    transpose_result(c - 1)
                if n < CHUNKS:
                    if place == KV_AT:
                        project_kv(n)
                    if place == Q_AT:
                        project_q(n)
                    if place in SCORE_AT:
                        scores(n, SCORE_AT.index(place))
                    if place in PROB_AT:
                        transpose_prob(n, PROB_AT.index(place))
                    if place in VALUE_AT:
                        weigh_values(n, VALUE_AT.index(place))
                    if place == PROJECT_AT:
                        project_out(n, range(ROWT))
                    if place == X2T_AT:
                        transpose_x2(n, range(ROWT))
                    if place == ROUTE_AT:
                        route(n)
                    if place == GATES_AT:
                        transpose_gates(n)
                if c == 0 and place == (0, 0):
                    transpose_gates(0)
                if place in GATED_AT:
                    broadcast_gate(c, GATED_AT.index(place))

            pe.wait_ge(qkv_in, 16)
            pe.wait_ge(xcol0_in, 16)
            project_q(0)
            project_kv(0)
            pe.wait_ge(setup_done, SETUP_STEPS)
            for s in range(SETS):
                scores(0, s)
            transpose_prob(0, 0)
            transpose_prob(0, 1)
            weigh_values(0, 0)
            transpose_prob(0, 2)
            weigh_values(0, 1)
            transpose_prob(0, 3)
            pe.wait_ge(proj_in, 16)
            for s in range(SETS):
                if s + 2 < SETS:
                    weigh_values(0, s + 2)
                project_out(0, [s])
            for j in range(ROWT):
                transpose_x2(0, [j])
            route(0)
            pe.wait_ge(xcols_in, 16)
            for c in range(CHUNKS):
                for t in range(TILES):
                    first_up(c, t)
                    beside(c, (t, 0))
                    second_up(c, t)
                    beside(c, (t, 1))
                    if t >= LAG:
                        down(c, t - LAG)
                    elif c > 0:
                        down(c - 1, TILES + t - LAG)
                    beside(c, (t, 2))
            for t in range(TILES - LAG, TILES):
                down(CHUNKS - 1, t)
            transpose_result(CHUNKS - 1)

        @block.scalar
        def _(act):
            act.dma_start(bias[:, :], biases).then_inc(const_in, 16)
            act.dma_start(cst[:, :], consts).then_inc(const_in, 16)
            act.dma_start(mask_f[:, :], masks).then_inc(mask_in, 16)
            act.dma_start(gsel_f, selectors).then_inc(gsel_in, 16)

            def queries(n):
                act.wait_ge(q_mm, n + 1)
                after(act, score_mm, SETS * n)
                for i in range(HPG):
                    rows = slice(GD * i, GD * (i + 1))
                    act.activation(qT[:, :, i, :], blocks(t_bank[rows, :], QB), ACT.Identity,
                                   bias=bias[rows, B_Q:B_Q + 1]).then_inc(q_sb, 1)

            def exps(n, s):
                act.wait_ge(shift_done, SETS * n + s + 1)
                act.activation(prob[:, s, :], shifted[:, s, :], ACT.Exp, scale=SCALE).then_inc(exp_done, 1)
                act.activation(esink[:, s, :], mrow[:, s, :], ACT.Exp, scale=-SCALE,
                               bias=bias[:, B_SINK:B_SINK + 1]).then_inc(esink_done, 1)

            def exps_together(n):
                act.wait_ge(shift_done, SETS * (n + 1))
                act.activation(prob[:, :, :], shifted[:, :, :], ACT.Exp, scale=SCALE).then_inc(exp_done, SETS)
                act.activation(esink[:, :, :], mrow[:, :, :], ACT.Exp, scale=-SCALE,
                               bias=bias[:, B_SINK:B_SINK + 1]).then_inc(esink_done, SETS)

            def own_values(n):
                act.wait_ge(v_sb, GROUPS * (n + 1))
                after(act, vbd_done, n)
                for g in range(GROUPS):
                    rows = 2 * g * GD
                    act.activation(vT[rows + GD:rows + 2 * GD, 0:CT], vT[rows:rows + GD, QB:QB + CT],
                                   ACT.Copy).then_inc(own_v_sb, 1)

            def prob_out(n, s):
                act.wait_ge(probT_mm, SETS * n + s + 1)
                after(act, pv_mm, SETS * n + max(s - 1, 0))
                act.activation(probT[:, s % 2, :], prob_bank(n, s)[:, :], ACT.Copy).then_inc(probT_sb, 1)

            def x2T_out(n):
                act.wait_ge(x2T_mm, ROWT * (n + 1))
                after(act, ysum_done, n - 1)
                act.activation(x2T[:, slot(n)], t_bank[:, :], ACT.Copy).then_inc(x2T_sb, 1)

            def router_tanh(n):
                act.wait_ge(lead_done, n + 1)
                act.activation(half[:, :], lead[:, :], ACT.Tanh, scale=0.5).then_inc(half_done, 1)

            def gates_out(n):
                act.wait_ge(gT_mm, n + 1)
                act.activation(gT[:, slot(n)], t_bank[0:2 * EXPERTS, :], ACT.Copy).then_inc(gT_sb, 1)

            def weights_out(lot):
                e0, e1 = WEIGHT_LOTS[lot]
                act.wait_ge(weights_in[lot], 32)
                act.activation(up_hi[:, e0:e1, :], up_f[:, e0:e1, :], ACT.Copy)
                act.activation(down_hi[:, e0:e1, :, :], down_f[:, e0:e1, :, :], ACT.Copy).then_inc(weights_hi, 1)

            def silu(c, t):
                at = TILES * c + t
                act.wait_ge(gate_mm, at + 1)
                after(act, h_done, at - 1)
                act.activation(sil[:, t % 2, :], gate_bank[t % 2][:, :], ACT.Silu).then_inc(silu_done, 1)

            def h_high(at):
                act.wait_ge(h_done, at + 1)
                after(act, down_mm, at - RING + 1)
                act.activation(hhi[:, at % RING, :], h[:, at % 2, :], ACT.Copy).then_inc(hhi_done, 1)

            def xg_high(c, e):
                act.wait_ge(xg_done, EXPERTS * c + e + 1)
                after(act, up_mm, TILES * c + (2 * e if e >= 2 else 0))
                act.activation(xghi[:, e % 2, :], xg[:, slot(e)], ACT.Copy).then_inc(xghi_done, 1)

            def beside(c, place):
                n = c + 1
                if n < CHUNKS:
                    if place == Q_AT:
                        queries(n)
                    if place == VBD_AT:
                        own_values(n)
                    if place == EXP_AT:
                        exps_together(n)
                    if place in PROB_AT:
                        prob_out(n, PROB_AT.index(place))
                    if place == X2T_AT:
                        x2T_out(n)
                    if place == WEIGHT_AT:
                        router_tanh(n)
                    if place == GATES_AT:
                        gates_out(n)
                if c == 0 and place == (0, 0):
                    gates_out(0)
                if place in GATED_HIGH_AT:
                    xg_high(c, GATED_HIGH_AT.index(place))
                if c == 0 and place in SPLIT_AT:
                    weights_out(2 + SPLIT_AT.index(place))

            act.wait_ge(exponent_done, 1)
            act.activation(warm[:, :], eps[:, :], ACT.Exp)
            act.wait_ge(const_in, 32)
            queries(0)
            own_values(0)
            exps(0, 0)
            exps(0, 1)
            prob_out(0, 0)
            exps(0, 2)
            prob_out(0, 1)
            exps(0, 3)
            prob_out(0, 2)
            weights_out(0)
            prob_out(0, 3)
            weights_out(1)
            x2T_out(0)
            router_tanh(0)
            for c in range(CHUNKS):
                for t in range(TILES):
                    silu(c, t)
                    beside(c, (t, 0))
                    if c + t > 0:
                        h_high(TILES * c + t - 1)
                    beside(c, (t, 1))
                    beside(c, (t, 2))
            h_high(TILES * CHUNKS - 1)

        @block.vector
        def _(dve):
            def keys(n):
                after(dve, score_mm, SETS * n)
                if n > 0:
                    dve.tensor_copy(kM[:, :, 0:QB], kM[:, :, CT:CT + QB]).then_inc(k_carried, 1)
                    dve.wait_ge(k_carried, n)
                dve.wait_ge(kv_mm, n + 1)
                for g in range(GROUPS):
                    dve.tensor_scalar(kM[:, g, QB:QB + CT], m_bank[0:GD, :], bias[0:GD, B_KV:B_KV + 1],
                                      cst[0:GD, C_GROUP + g:C_GROUP + g + 1],
                                      ALU.add, ALU.mult).then_inc(k_sb, 1)

            def values(n):
                if n > 0:
                    dve.wait_ge(vbd_done, n)
                    for g in range(GROUPS):
                        rows = slice(2 * g * GD, (2 * g + 1) * GD)
                        dve.tensor_copy(vT[rows, 0:QB], vT[rows, CT:CT + QB]).then_inc(v_carried, 1)
                    dve.wait_ge(v_carried, GROUPS * n)
                here = slice(GD, 2 * GD)
                for g in range(GROUPS):
                    dve.tensor_scalar(vT[2 * g * GD:(2 * g + 1) * GD, QB:QB + CT], m_bank[here, :],
                                      bias[here, B_KV:B_KV + 1], cst[here, C_GROUP + g:C_GROUP + g + 1],
                                      ALU.add, ALU.mult).then_inc(v_sb, 1)

            def value_blocks(n):
                dve.wait_ge(v_sb, GROUPS * (n + 1))
                dve.wait_ge(own_v_sb, GROUPS * (n + 1))
                after(dve, pv_mm, SETS * n)
                dve.transpose(blocks(vbd[:, 0:BLOCKS * VW], VW)[:, :, 0:GD],
                              blocks(vT[:, 0:CT], QB)).then_inc(vbd_done, 1)

            def softmax_shift(n, s):
                at = SETS * n + s + 1
                by_row = "p (i k) -> p i k"
                dve.wait_ge(score_mm, at)
                dve.tensor_reduce(mx[:, s, :], score_bank(n, s)[:, :].rearrange(by_row, k=2 * QB),
                                  AX.X, ALU.max).then_inc(max_done, 1)
                dve.wait_ge(max_done, at)
                dve.tensor_scalar(mrow[:, s, :], mx[:, s, :], sink4[:, :], None, ALU.max).then_inc(mrow_done, 1)
                dve.wait_ge(mrow_done, at)
                dve.tensor_tensor(shifted[:, s, :].rearrange(by_row, k=2 * QB),
                                  score_bank(n, s)[:, :].rearrange(by_row, k=2 * QB),
                                  mrow[:, s, :].unsqueeze(2).to_broadcast([P, BPG * GROUPS, 2 * QB]),
                                  ALU.subtract).then_inc(shift_done, 1)

            def normalise(n, s):
                at = SETS * n + s + 1
                weighed = blocks(value_bank(n, s)[:, :], P)
                by_group = "p (b g) -> p b g"
                dve.wait_ge(esink_done, at)
                dve.wait_ge(pv_mm, at)
                dve.tensor_tensor(den[:, s, :].rearrange(by_group, b=BPG), weighed[:, :, GD:VW],
                                  esink[:, s, :].rearrange(by_group, b=BPG), ALU.add).then_inc(den_done, 1)
                dve.wait_ge(den_done, at)
                dve.reciprocal(rden[:, s, :], den[:, s, :]).then_inc(rden_done, 1)
                dve.wait_ge(rden_done, at)
                dve.tensor_tensor(o[:, sets[s]].rearrange("p (b g d) -> p b g d", b=BPG, g=GROUPS),
                                  weighed[:, :, 0:GD].rearrange("p b (g d) -> p b g d", g=GROUPS),
                                  rden[:, s, :].rearrange(by_group, b=BPG).unsqueeze(3)
                                  .to_broadcast([P, BPG, GROUPS, HD]), ALU.mult).then_inc(o_done, 1)

            def turn(n, tiles):
                some = slice(tiles[0] * P, (tiles[-1] + 1) * P)
                dve.wait_ge(o_done, SETS * n + tiles[-1] + 1)
                after(dve, proj_mm, ROWT * n)
                dve.transpose(oT[:, some], o[:, some]).then_inc(oT_done, len(tiles))

            def norm1(n, tiles):
                at = ROWT * n + tiles[-1] + 1
                some = slice(tiles[0], tiles[-1] + 1)
                dve.wait_ge(proj_mm, at)
                dve.wait_ge(xbias_done, 1 if n == 0 else 2)
                dve.tensor_tensor(res[:, some, :], blocks(project_bank(n, tiles[0])[:, :], D)[:, some, :],
                                  xr[:, n * ROWT + tiles[0]:n * ROWT + tiles[-1] + 1, :],
                                  ALU.add).then_inc(res_done, len(tiles))
                dve.wait_ge(res_done, at)
                for j in tiles:
                    dve.bn_stats(bn1[:, j, :], res[:, j, :]).then_inc(bn1_done, 1)
                dve.wait_ge(bn1_done, at)
                for j in tiles:
                    dve.bn_aggr(mv1[:, j, :], bn1[:, j, :]).then_inc(mv1_done, 1)

            def scale1(n, tiles):
                dve.wait_ge(rstd1_done, ROWT * n + tiles[-1] + 1)
                for j in tiles:
                    dve.tensor_scalar(x2[:, j, :], res[:, j, :], mv1[:, j, 0:1], rstd1[:, j:j + 1],
                                      ALU.subtract, ALU.mult).then_inc(x2_done, 1)

            def x2_high(n):
                dve.wait_ge(x2T_sb, n + 1)
                dve.tensor_copy(x2hi[:, slot(n)], x2T[:, slot(n)]).then_inc(x2hi_done, 1)

            def logits(n):
                every = [P, ROWT, EXPERTS]
                dve.wait_ge(router_mm, n + 1)
                dve.tensor_tensor(logit[:, :, :], blocks(m_bank[:, :], P)[:, :, 0:EXPERTS],
                                  bias[:, B_R:B_R + EXPERTS].unsqueeze(1).to_broadcast(every),
                                  ALU.add).then_inc(logit_done, 1)
                dve.wait_ge(logit_done, n + 1)
                for j in range(ROWT):
                    ins = dve.max(top[:, j, :], logit[:, j, :])
                ins.then_inc(top_done, 1)
                dve.wait_ge(top_done, n + 1)
                dve.tensor_tensor(lead[:, :], top[:, :, 0], top[:, :, 1], ALU.subtract).then_inc(lead_done, 1)
                for j in range(ROWT):
                    ins = dve.max_index(topi[:, j, :], top[:, j, :], logit[:, j, :])
                ins.then_inc(topi_done, 1)
                dve.wait_ge(topi_done, n + 1)
                dve.tensor_copy(topf[:, :, :], topi[:, :, 0:2]).then_inc(topf_done, 1)
                dve.wait_ge(topf_done, n + 1)
                for i in range(2):
                    ins = dve.tensor_tensor(pick[:, i, :, :],
                                            cst[:, C_IOTA:C_IOTA + EXPERTS].unsqueeze(1).to_broadcast(every),
                                            topf[:, :, i:i + 1].to_broadcast(every), ALU.is_equal)
                ins.then_inc(pick_done, 1)
                dve.wait_ge(pick_done, n + 1)
                dve.tensor_tensor(signed[:, :, :], pick[:, 0, :, :], pick[:, 1, :, :], ALU.subtract)
                dve.tensor_tensor(picked[:, :, :], pick[:, 0, :, :], pick[:, 1, :, :], ALU.add)\
                   .then_inc(picked_done, 1)
                dve.wait_ge(picked_done, n + 1)
                dve.tensor_scalar(picked[:, :, :], picked[:, :, :], 0.5, None, ALU.mult).then_inc(halved_done, 1)

            def gates(n):
                every = [P, ROWT, EXPERTS]
                dve.wait_ge(half_done, n + 1)
                dve.wait_ge(halved_done, n + 1)
                dve.tensor_tensor(swing[:, :, :], signed[:, :, :], half[:, :].unsqueeze(2).to_broadcast(every),
                                  ALU.mult).then_inc(swing_done, 1)
                dve.wait_ge(swing_done, n + 1)
                dve.scalar_tensor_tensor(gate[:, :, :], swing[:, :, :], 0.5, picked[:, :, :],
                                         ALU.mult, ALU.add).then_inc(gate_done, 1)
                dve.wait_ge(gate_done, n + 1)
                dve.tensor_copy(gparts[:, :, 0:EXPERTS], gate[:, :, :]).then_inc(ghi_done, 1)
                dve.wait_ge(ghi_done, n + 1)
                dve.tensor_tensor(gparts[:, :, EXPERTS:2 * EXPERTS], gate[:, :, :],
                                  gparts[:, :, 0:EXPERTS].bitcast(F32), ALU.subtract).then_inc(gparts_done, 1)

            def gated_input(c, e):
                dve.wait_ge(gcast_mm, EXPERTS * c + e + 1)
                after(dve, xglo_done, EXPERTS * c + e - 1)
                dve.tensor_tensor(xg[:, slot(e)], x2T[:, slot(c)], s_bank[:, :], ALU.mult)\
                   .then_inc(xg_done, 1)

            def xg_low(c, e):
                dve.wait_ge(xghi_done, EXPERTS * c + e + 1)
                dve.wait_ge(xglo_done, EXPERTS * c + e)
                dve.tensor_tensor(xglo[:, e % 2, :], xg[:, slot(e)], xghi[:, e % 2, :].bitcast(F32),
                                  ALU.subtract).then_inc(xglo_done, 1)

            def hidden(c, t):
                at = TILES * c + t
                dve.wait_ge(silu_done, at + 1)
                dve.wait_ge(up_mm, at + 1)
                after(dve, hlo_done, at - 1)
                dve.tensor_tensor(h[:, t % 2, :], sil[:, t % 2, :], up_bank[t % 2][:, :], ALU.mult)\
                   .then_inc(h_done, 1)

            def sum_y(c):
                dve.wait_ge(down_mm, TILES * (c + 1))
                after(dve, yT_mm, c)
                dve.tensor_tensor(ysum[:, :], x2T[:, slot(c)], y_bank[:, :], ALU.add).then_inc(ysum_done, 1)

            def stats2(c):
                dve.wait_ge(yT_mm, c + 1)
                for j in range(ROWT):
                    ins = dve.bn_stats(bn2[:, j, :], t_bank[:, j * D:(j + 1) * D])
                ins.then_inc(bn2_done, 1)
                dve.wait_ge(bn2_done, c + 1)
                for j in range(ROWT):
                    ins = dve.bn_aggr(mv2[:, j, :], bn2[:, j, :])
                ins.then_inc(mv2_done, 1)

            def scale2(c):
                dve.wait_ge(rstd2_done, c + 1)
                after(dve, stored, 16 * c)
                for j in range(ROWT):
                    ins = dve.tensor_scalar(result[:, j, :], t_bank[:, j * D:(j + 1) * D],
                                            mv2[:, j, 0:1], rstd2[:, j:j + 1], ALU.subtract, ALU.mult)
                ins.then_inc(result_done, 1)

            def weights_low(lot):
                e0, e1 = WEIGHT_LOTS[lot]
                dve.wait_ge(weights_hi, lot + 1)
                dve.wait_ge(weights_lo, lot)
                dve.tensor_tensor(up_lo[:, e0:e1, :], up_f[:, e0:e1, :], up_hi[:, e0:e1, :].bitcast(F32),
                                  ALU.subtract)
                dve.tensor_tensor(down_lo[:, e0:e1, :, :], down_f[:, e0:e1, :, :],
                                  down_hi[:, e0:e1, :, :].bitcast(F32), ALU.subtract).then_inc(weights_lo, 1)

            def beside(c, place):
                n = c + 1
                if n < CHUNKS:
                    if place == KV_AT:
                        keys(n)
                        values(n)
                    if place == VBD_AT:
                        value_blocks(n)
                    if place in SCORE_AT:
                        softmax_shift(n, SCORE_AT.index(place))
                    if place in VALUE_AT:
                        normalise(n, VALUE_AT.index(place))
                    if place == VALUE_AT[SETS - 1]:
                        turn(n, range(ROWT))
                    if place == PROJECT_AT:
                        norm1(n, range(ROWT))
                    if place == SCALE_AT:
                        scale1(n, range(ROWT))
                    if place == X2T_AT:
                        x2_high(n)
                    if place == ROUTE_AT:
                        logits(n)
                    if place == WEIGHT_AT:
                        gates(n)
                if place in GATED_AT:
                    gated_input(c, GATED_AT.index(place))
                if place == RESULT_AT and c > 0:
                    stats2(c - 1)
                if place == STORE_AT and c > 0:
                    scale2(c - 1)
                if c == 0 and place in SPLIT_LOW_AT:
                    weights_low(2 + SPLIT_LOW_AT.index(place))

            dve.memset(vbd[:, :], 0.0).then_inc(setup_done, 1)
            dve.memset(kM[:, :, 0:QB], 0.0).then_inc(setup_done, 1)
            dve.memset(vT[:, :], 0.0).then_inc(setup_done, 1)
            dve.wait_ge(const_in, 32)
            dve.tensor_scalar(sink4[:, :], bias[:, B_SINK:B_SINK + 1], FP16_MIN, 1.0 / SCALE,
                              ALU.max, ALU.mult).then_inc(setup_done, 1)
            dve.wait_ge(setup_done, 3)
            dve.tensor_copy(blocks(vbd[:, 0:BLOCKS * VW], VW)[:, :, GD:VW],
                            cst[:, C_DEN:C_DEN + GROUPS].unsqueeze(1).to_broadcast([P, BLOCKS, GROUPS]))\
               .then_inc(setup_done, 1)
            dve.wait_ge(mask_in, 16)
            dve.tensor_copy(mask[:, :], mask_f[:, :]).then_inc(setup_done, 1)
            dve.wait_ge(gsel_in, 16)
            dve.tensor_copy(gsel[:, :], gsel_f).then_inc(setup_done, 1)
            keys(0)
            dve.wait_ge(setup_done, SETUP_STEPS)
            values(0)
            softmax_shift(0, 0)
            value_blocks(0)
            for s in range(1, SETS):
                softmax_shift(0, s)
            for s in range(SETS):
                normalise(0, s)
                turn(0, [s])
                if s > 0:
                    norm1(0, [s - 1])
            norm1(0, [ROWT - 1])
            for j in range(ROWT):
                scale1(0, [j])
            x2_high(0)
            dve.wait_ge(x2hi_done, 1)
            dve.tensor_tensor(x2lo[:, slot(0)], x2T[:, slot(0)], x2hi[:, slot(0)].bitcast(F32),
                              ALU.subtract).then_inc(x2lo_done, 1)
            logits(0)
            gates(0)
            for c in range(CHUNKS):
                for t in range(TILES):
                    if t == LAG and c > 0:
                        sum_y(c - 1)
                    beside(c, (t, 0))
                    hidden(c, t)
                    beside(c, (t, 1))
                    beside(c, (t, 2))
                    if c == CHUNKS - 1 and (t, 0) in GATED_HIGH_AT:
                        xg_low(c, GATED_HIGH_AT.index((t, 0)))
            sum_y(CHUNKS - 1)
            stats2(CHUNKS - 1)
            scale2(CHUNKS - 1)

        @block.gpsimd
        def _(pool):
            def rstd1_of(n, tiles):
                at = ROWT * n + tiles[-1] + 1
                some = slice(tiles[0], tiles[-1] + 1)
                pool.wait_ge(mv1_done, at)
                pool.tensor_tensor(vareps1[:, some], mv1[:, some, 1], eps[:, some], ALU.add)\
                    .then_inc(vareps1_done, len(tiles))
                pool.wait_ge(vareps1_done, at)
                pool.tensor_tensor(rstd1[:, some], vareps1[:, some], exponent[:, some], ALU.pow)\
                    .then_inc(rstd1_done, len(tiles))

            def rstd2_of(c):
                pool.wait_ge(mv2_done, c + 1)
                pool.tensor_tensor(vareps2[:, :], mv2[:, :, 1], eps[:, :], ALU.add).then_inc(vareps2_done, 1)
                pool.wait_ge(vareps2_done, c + 1)
                pool.tensor_tensor(rstd2[:, :], vareps2[:, :], exponent[:, :], ALU.pow).then_inc(rstd2_done, 1)

            def x2_low(n):
                pool.wait_ge(x2hi_done, n + 1)
                pool.tensor_tensor(x2lo[:, slot(n)], x2T[:, slot(n)], x2hi[:, slot(n)].bitcast(F32),
                                   ALU.subtract).then_inc(x2lo_done, 1)

            def h_low(at):
                pool.wait_ge(hhi_done, at + 1)
                pool.tensor_tensor(hlo[:, at % RING, :], h[:, at % 2, :], hhi[:, at % RING, :].bitcast(F32),
                                   ALU.subtract).then_inc(hlo_done, 1)

            def xg_low(c, e):
                pool.wait_ge(xghi_done, EXPERTS * c + e + 1)
                pool.tensor_tensor(xglo[:, e % 2, :], xg[:, slot(e)], xghi[:, e % 2, :].bitcast(F32),
                                   ALU.subtract).then_inc(xglo_done, 1)

            def add_bias(first, last):
                some = xr[:, first:last, :]
                pool.tensor_tensor(some, some, bias[:, B_O:B_O + D].unsqueeze(1)
                                   .to_broadcast([P, last - first, D]), ALU.add).then_inc(xbias_done, 1)

            def weights_low(lot):
                e0, e1 = WEIGHT_LOTS[lot]
                pool.wait_ge(weights_hi, lot + 1)
                pool.tensor_tensor(up_lo[:, e0:e1, :], up_f[:, e0:e1, :], up_hi[:, e0:e1, :].bitcast(F32),
                                   ALU.subtract)
                pool.tensor_tensor(down_lo[:, e0:e1, :, :], down_f[:, e0:e1, :, :],
                                   down_hi[:, e0:e1, :, :].bitcast(F32), ALU.subtract).then_inc(weights_lo, 1)

            def beside(c, place):
                n = c + 1
                if place in GATED_HIGH_AT and c < CHUNKS - 1:
                    xg_low(c, GATED_HIGH_AT.index(place))
                if place == RESULT_AT and c > 0:
                    rstd2_of(c - 1)
                if n < CHUNKS:
                    if place == PROJECT_AT:
                        rstd1_of(n, range(ROWT))
                    if place == X2T_AT:
                        x2_low(n)
                if c == 0 and place == (8, 0):
                    pool.wait_ge(xrows_in, 16)
                    add_bias(ROWT, CHUNKS * ROWT)

            pool.memset(eps[:, :], LN_EPS).then_inc(exponent_done, 1)
            pool.memset(exponent[:, :], -0.5).then_inc(exponent_done, 1)
            pool.wait_ge(const_in, 32)
            pool.wait_ge(xrow0_in, 16)
            add_bias(0, ROWT)
            pool.wait_ge(exponent_done, 2)
            weights_low(0)
            for j in range(ROWT):
                rstd1_of(0, [j])
            weights_low(1)
            for c in range(CHUNKS):
                for t in range(TILES):
                    if c + t > 0:
                        h_low(TILES * c + t - 1)
                    for place in range(3):
                        beside(c, (t, place))
            h_low(TILES * CHUNKS - 1)
            rstd2_of(CHUNKS - 1)


def kernel(L0_attn_x, L0_attn_sink_bias, L0_attn_Wq, L0_attn_bq, L0_attn_Wk, L0_attn_bk, L0_attn_Wv,
           L0_attn_bv, L0_attn_Wo, L0_attn_bo, L0_ffn_sw1, L0_ffn_sw2, L0_ffn_sw3, L0_ffn_ew1,
           L0_ffn_ew2, L0_ffn_ew3, L0_ffn_rw, L0_ffn_rb):
    import numpy as np
    import concourse.bacc as bacc
    from concourse.bass_utils import run_bass_kernel_spmd

    def arr(a):
        return np.asarray(a)

    x = arr(L0_attn_x).reshape(TOKENS, D)

    def rows_by_head(a):
        a = arr(a)
        return a.reshape(GROUPS, HPG, HD, *a.shape[1:]).swapaxes(0, 1).reshape(a.shape)

    router = np.zeros((D, P), np.float32)
    router[:, 0:EXPERTS] = arr(L0_ffn_rw)
    proj = np.concatenate([rows_by_head(L0_attn_Wq).T, arr(L0_attn_Wk).T, arr(L0_attn_Wv).T,
                           rows_by_head(arr(L0_attn_Wo).T), router], axis=1)

    bias = np.zeros((P, B_END), np.float32)
    bias[:, B_Q] = rows_by_head(L0_attn_bq)
    bias[0:2 * GD, B_KV] = np.concatenate([arr(L0_attn_bk), arr(L0_attn_bv)])
    bias[:, B_SINK] = arr(L0_attn_sink_bias)
    bias[:, B_R:B_R + EXPERTS] = arr(L0_ffn_rb)
    bias[:, B_O:B_O + D] = arr(L0_attn_bo)

    up = np.concatenate([np.concatenate([arr(L0_ffn_sw1)[None], arr(L0_ffn_ew1)]),
                         np.concatenate([arr(L0_ffn_sw2)[None], arr(L0_ffn_ew2)])], axis=2)
    up = up.transpose(1, 0, 2)
    down = np.concatenate([arr(L0_ffn_sw3)[None], arr(L0_ffn_ew3)])
    down = down.reshape(FFNS, 2, P, D).transpose(2, 0, 1, 3)

    row = np.arange(P)
    c = np.zeros((P, C_END), np.float32)
    c[:, C_ID:C_ID + P] = np.eye(P)
    c[:, C_IOTA:C_IOTA + EXPERTS] = np.arange(EXPERTS)
    for g in range(GROUPS):
        c[:, C_DEN + g] = row // (2 * QB) == g
        c[:, C_GROUP + g] = (row % GD) // HD == g
    q, k = np.arange(QB)[:, None], np.arange(QB)[None, :]
    before = np.where(k > q, 0.0, MASKED)
    own = np.where(k <= q, 0.0, MASKED)
    first = [np.full((QB, QB), MASKED), own] * GROUPS
    mask = np.concatenate([np.tile(np.eye(QB), (1, HPG))] + first + [before, own] * GROUPS * BPG,
                          axis=1).astype(np.float32)
    select = np.tile(np.repeat(np.eye(EXPERTS, dtype=np.float32), P, axis=1), (2, 1))

    feeds = {"x_cols": x.T, "x_rows": x, "proj_w": proj, "biases": bias, "consts": c,
             "masks": mask, "selectors": select,
             "up_w": up, "down_w": down}
    feeds = {name: np.ascontiguousarray(a) for name, a in feeds.items()}
    nc = bacc.Bacc("TRN2", target_bir_lowering=False, num_devices=1)
    args = [nc.dram_tensor(name, a.shape, mybir.dt.from_np(a.dtype), kind="ExternalInput").ap()
            for name, a in feeds.items()]
    result = nc.dram_tensor("out", (TOKENS, D), F32, kind="ExternalOutput").ap()
    build(nc, *args, result)
    run = run_bass_kernel_spmd(nc, [feeds], core_ids=[0])
    return run.results[0]["out"].reshape(arr(L0_attn_x).shape)
```

```python
from contextlib import ExitStack

import concourse.bass as bass
from concourse import mybir

ALU = mybir.AluOpType
ACT = mybir.ActivationFunctionType
AX = mybir.AxisListType
F32 = mybir.dt.float32
F32R = mybir.dt.float32r
BF16 = mybir.dt.bfloat16
U32 = mybir.dt.uint32

P = 128
D = 128
TOKENS = 2048
HEADS, GROUPS, HD = 8, 2, 16
HPG = HEADS // GROUPS
GD = GROUPS * HD
WIN = 32
EXPERTS = 8
FFNS = EXPERTS + 1
HIDDEN = 256
CT = 512
CHUNKS = TOKENS // CT
CHUNKS_PER_SEQUENCE = 2
ROWT = CT // P
QB = 32
BLOCKS = CT // QB
BPG = P // GD
SETS = BLOCKS // BPG
TILES = FFNS * HIDDEN // P
LAG = 3
RING = 4
MROWS = GD + 2 * QB
VW = GD + GROUPS
LN_EPS = 1e-5
SCALE = float(HD) ** -0.5
FP16_MIN = -65504.0
MASKED = -262144.0

C_ID = 0
C_IOTA = C_ID + P
C_DEN = C_IOTA + EXPERTS
C_GROUP = C_DEN + GROUPS
C_END = C_GROUP + GROUPS

W_Q = 0
W_KV = W_Q + P
W_QKV = W_KV + 2 * GD
W_O = W_QKV
W_R = W_O + P
W_END = W_R + P

B_Q, B_KV, B_SINK, B_R, B_O = 0, 1, 2, 3, 3 + EXPERTS
B_END = B_O + D

WEIGHT_LOTS = [(0, 1), (1, 3), (3, 6), (6, 9)]
FIRST_OF_LOT = {2 * e0: lot for lot, (e0, _) in enumerate(WEIGHT_LOTS)}

KV_AT = (1, 0)
Q_AT = (1, 0)
SCORE_AT = [(2, 1), (3, 1), (4, 2), (6, 0)]
PROB_AT = [(9, 0), (9, 1), (10, 1), (10, 2)]
VALUE_AT = [(9, 1), (10, 1), (11, 0), (11, 2)]
PROJECT_AT = (12, 2)
X2T_AT = (15, 1)
ROUTE_AT = (16, 0)
GATES_AT = (17, 2)
GATED_AT = [(0, 2), (1, 1), (2, 2), (5, 1), (8, 0), (9, 2), (11, 2), (14, 0)]
RESULT_AT = (3, 2)
QUERIES_AT = (1, 2)
OWN_VALUES_AT = (5, 0)
EXP_AT = (7, 0)
PROB_OUT_AT = [(7, 1), (8, 1), (10, 0), (10, 2)]
X2T_OUT_AT = (14, 2)
TANH_AT = (15, 1)
GATES_OUT_AT = (17, 0)
GATED_HIGH_AT = [(1, 0), (2, 0), (4, 0), (6, 0), (7, 2), (10, 0), (12, 1), (14, 0)]
SPLIT_AT = [(0, 1), (1, 0)]
KEYS_AT = (0, 1)
VALUES_AT = (0, 1)
VBD_AT = (6, 2)
SHIFT_AT = [(2, 0), (3, 1), (4, 1), (6, 0)]
NORMALISE_AT = [(9, 0), (9, 2), (10, 2), (11, 1)]
TURN_AT = (11, 2)
NORM_AT = (12, 1)
SCALE_AT = (14, 0)
X2_HIGH_AT = (15, 2)
PICK_AT = (15, 2)
WEIGHT_AT = (15, 2)
GATED_INPUT_AT = [(0, 0), (0, 2), (3, 1), (5, 2), (7, 0), (9, 0), (12, 0), (13, 1)]
STATS_AT = (4, 0)
STORE_AT = (6, 2)
SPLIT_LOW_AT = [(0, 1), (7, 1)]
RSTD1_AT = (12, 2)
X2_LOW_AT = (15, 2)
RSTD2_AT = (5, 0)
GATED_LOW_AT = [(0, 0), (2, 0), (3, 0), (5, 0), (7, 0), (9, 0), (12, 0), (14, 0)]
RESIDUAL_AT = (11, 2)

GATES_0_AT = (0, 1)
GATED_INPUT_0_AT = (0, 1)

HURRY_FROM = TILES * CHUNKS - 3

WARM_UP = 6

SETUP_STEPS = 6


def build(nc, x_cols, x_rows, proj_w, biases, consts, masks, selectors, up_w, down_w, out):
    ctx = ExitStack()
    with ctx:
        def sb(name, shape, dt=F32):
            return ctx.enter_context(nc.sbuf_tensor(name, shape, dt))

        def bank(name):
            return ctx.enter_context(nc.psum_tensor(name, [P, CT], F32))

        def sem(name):
            return ctx.enter_context(nc.semaphore(name))

        cst = sb("cst", [P, C_END])
        pw = sb("pw", [P, W_END])
        bias = sb("bias", [P, B_END])
        xT = sb("xT", [P, TOKENS])
        xr = sb("xr", [P, CHUNKS * ROWT, D])
        up_f = sb("up_f", [P, FFNS, 2 * HIDDEN])
        down_f = sb("down_f", [P, FFNS, 2, D])
        up_hi = sb("up_hi", [P, FFNS, 2 * HIDDEN], F32R)
        up_lo = sb("up_lo", [P, FFNS, 2 * HIDDEN], F32R)
        down_hi = sb("down_hi", [P, FFNS, 2, D], F32R)
        down_lo = sb("down_lo", [P, FFNS, 2, D], F32R)
        gsel = sb("gsel", [2 * EXPERTS, EXPERTS * P], F32R)
        eps = sb("eps", [P, ROWT])
        exponent = sb("exponent", [P, ROWT])
        sink4 = sb("sink4", [P, 1])
        idle = sb("idle", [P, CT], BF16)
        warm = sb("warm", [P, ROWT])
        qT = sb("qT", [MROWS, BLOCKS, HPG, QB])
        kM = sb("kM", [MROWS, GROUPS, QB + CT])
        vT = sb("vT", [P, QB + CT])
        vbd = sb("vbd", [P, BLOCKS * VW + P])
        mx = sb("mx", [P, SETS, BPG * GROUPS])
        mrow = sb("mrow", [P, SETS, BPG * GROUPS])
        shifted = sb("shifted", [P, SETS, CT])
        prob = shifted
        probT = sb("probT", [P, 2, CT])
        esink = sb("esink", [P, SETS, BPG * GROUPS])
        den = sb("den", [P, SETS, BPG * GROUPS])
        rden = sb("rden", [P, SETS, BPG * GROUPS])
        o = sb("o", [P, CT])
        oT = sb("oT", [P, CT])
        res = sb("res", [P, ROWT, D])
        bn1 = sb("bn1", [P, ROWT, 6])
        mv1 = sb("mv1", [P, ROWT, 2])
        vareps1 = sb("vareps1", [P, ROWT])
        rstd1 = sb("rstd1", [P, ROWT])
        x2 = sb("x2", [P, ROWT, D])
        x2T = sb("x2T", [P, 2 * CT])
        x2hi = sb("x2hi", [P, 2 * CT], F32R)
        x2lo = sb("x2lo", [P, 2 * CT], F32R)
        logit = sb("logit", [P, ROWT, EXPERTS])
        top = sb("top", [P, ROWT, 8])
        topi = sb("topi", [P, ROWT, 8], U32)
        topf = sb("topf", [P, ROWT, 2])
        pick = sb("pick", [P, 2, ROWT, EXPERTS])
        picked = sb("picked", [P, ROWT, EXPERTS])
        signed = sb("signed", [P, ROWT, EXPERTS])
        lead = sb("lead", [P, ROWT])
        half = sb("half", [P, ROWT])
        swing = sb("swing", [P, ROWT, EXPERTS])
        gate = sb("gate", [P, ROWT, EXPERTS])
        gparts = sb("gparts", [P, ROWT, 2 * EXPERTS], F32R)
        gT = sb("gT", [2 * EXPERTS, 2 * CT], F32R)
        xg = sb("xg", [P, 2 * CT])
        gsel_f = xg[0:2 * EXPERTS, 0:EXPERTS * P]
        xghi = sb("xghi", [P, 2, CT], F32R)
        xglo = sb("xglo", [P, 2, CT], F32R)
        sil = sb("sil", [P, 2, CT])
        h = sb("h", [P, 2, CT])
        hhi = sb("hhi", [P, RING, CT], F32R)
        hlo = sb("hlo", [P, RING, CT], F32R)
        ysum = sb("ysum", [P, CT])
        bn2 = sb("bn2", [P, ROWT, 6])
        mv2 = sb("mv2", [P, ROWT, 2])
        vareps2 = sb("vareps2", [P, ROWT])
        rstd2 = sb("rstd2", [P, ROWT])
        result = sb("result", [P, ROWT, D])

        gate_bank = [bank("gate_bank0"), bank("gate_bank1")]
        up_bank = [bank("up_bank0"), bank("up_bank1")]
        y_bank = bank("y_bank")
        s_bank = bank("s_bank")
        t_bank = bank("t_bank")
        m_bank = bank("m_bank")

        def score_bank(n, s):
            return m_bank if n > 0 else [s_bank, gate_bank[0], gate_bank[1], y_bank][s]

        def prob_bank(n, s):
            return t_bank if n > 0 else [t_bank, up_bank[0]][s % 2]

        def value_bank(n, s):
            return m_bank if n > 0 else [m_bank, up_bank[1]][s % 2]

        def query_bank(n):
            return up_bank[0] if n == 1 else t_bank

        def router_bank(n):
            return gate_bank[1] if n == 0 else m_bank

        def project_bank(n, j):
            return m_bank if n > 0 else score_bank(n, j)

        def result_bank(c, j):
            return t_bank if c < CHUNKS - 1 else [t_bank, m_bank, s_bank, gate_bank[0]][j]

        const_in = sem("const_in")
        mask_in = sem("mask_in")
        gsel_in = sem("gsel_in")
        qkv_in = sem("qkv_in")
        proj_in = sem("proj_in")
        xcol0_in = sem("xcol0_in")
        xcol1_in = sem("xcol1_in")
        xcols_in = sem("xcols_in")
        xrow0_in = sem("xrow0_in")
        xrows_in = sem("xrows_in")
        weights_in = [sem(f"weights_in{n}") for n in range(len(WEIGHT_LOTS))]
        setup_done = sem("setup_done")
        weights_hi = sem("weights_hi")
        weights_lo = sem("weights_lo")
        picks_cleared = sem("picks_cleared")
        even_picks_done = sem("even_picks_done")
        odd_picks_done = sem("odd_picks_done")
        xbias_done = sem("xbias_done")
        idle_done = sem("idle_done")
        exponent_done = sem("exponent_done")
        q_mm, kv_mm = sem("q_mm"), sem("kv_mm")
        q_sb = sem("q_sb")
        k_carried = sem("k_carried")
        halo_done = sem("halo_done")
        k_sb = sem("k_sb")
        v_carried = sem("v_carried")
        v_sb = sem("v_sb")
        own_v_sb = sem("own_v_sb")
        vbd_done = sem("vbd_done")
        score_mm = sem("score_mm")
        max_done = sem("max_done")
        mrow_done = sem("mrow_done")
        shift_done = sem("shift_done")
        exp_done = sem("exp_done")
        esink_done = sem("esink_done")
        probT_mm = sem("probT_mm")
        probT_sb = sem("probT_sb")
        pv_mm = sem("pv_mm")
        den_done = sem("den_done")
        rden_done = sem("rden_done")
        o_done = sem("o_done")
        oT_done = sem("oT_done")
        proj_mm = sem("proj_mm")
        res_done = sem("res_done")
        bn1_done = sem("bn1_done")
        mv1_done = sem("mv1_done")
        vareps1_done = sem("vareps1_done")
        rstd1_done = sem("rstd1_done")
        x2_done = sem("x2_done")
        x2T_mm = sem("x2T_mm")
        x2T_sb = sem("x2T_sb")
        x2hi_done = sem("x2hi_done")
        x2lo_done = sem("x2lo_done")
        router_mm = sem("router_mm")
        logit_done = sem("logit_done")
        top_done = sem("top_done")
        topi_done = sem("topi_done")
        topf_done = sem("topf_done")
        pick_done = sem("pick_done")
        picked_done = sem("picked_done")
        lead_done = sem("lead_done")
        half_done = sem("half_done")
        halved_done = sem("halved_done")
        swing_done = sem("swing_done")
        gate_done = sem("gate_done")
        ghi_done = sem("ghi_done")
        gparts_done = sem("gparts_done")
        gT_mm = sem("gT_mm")
        gT_sb = sem("gT_sb")
        gcast_mm = sem("gcast_mm")
        xg_done = sem("xg_done")
        xghi_done = sem("xghi_done")
        xglo_done = sem("xglo_done")
        gate_mm = sem("gate_mm")
        up_mm = sem("up_mm")
        silu_done = sem("silu_done")
        h_done = sem("h_done")
        hhi_done = sem("hhi_done")
        hlo_done = sem("hlo_done")
        down_mm = sem("down_mm")
        ysum_done = sem("ysum_done")
        yT_mm = sem("yT_mm")
        bn2_done = sem("bn2_done")
        mv2_done = sem("mv2_done")
        vareps2_done = sem("vareps2_done")
        rstd2_done = sem("rstd2_done")
        result_done = sem("result_done")
        stored = sem("stored")

        def tokens(n):
            return slice(n * CT, (n + 1) * CT)

        def slot(n):
            return slice((n % 2) * CT, (n % 2 + 1) * CT)

        def after(eng, semaphore, count):
            if count > 0:
                eng.wait_ge(semaphore, count)

        def blocks(ap, width):
            return ap.rearrange("p (b w) -> p b w", w=width)

        sets = [slice(s * BPG * QB, (s + 1) * BPG * QB) for s in range(SETS)]
        block = ctx.enter_context(nc.Block())

        @block.sync
        def _(sp):
            rows = x_rows.rearrange("(t p) d -> p t d", p=P)
            sp.dma_start(pw[:, 0:W_QKV], proj_w[:, 0:W_QKV]).then_inc(qkv_in, 16)
            sp.dma_start(xT[:, 0:CT], x_cols[:, 0:CT]).then_inc(xcol0_in, 16)
            sp.dma_start(pw[:, W_QKV:W_END], proj_w[:, W_QKV:W_END]).then_inc(proj_in, 16)
            sp.dma_start(xr[:, 0:ROWT, :], rows[:, 0:ROWT, :]).then_inc(xrow0_in, 16)
            for n, (e0, e1) in enumerate(WEIGHT_LOTS):
                if n == 2:
                    sp.dma_start(xT[:, CT:2 * CT], x_cols[:, CT:2 * CT]).then_inc(xcol1_in, 16)
                sp.dma_start(up_f[:, e0:e1, :], up_w[:, e0:e1, :]).then_inc(weights_in[n], 16)
                sp.dma_start(down_f[:, e0:e1, :, :], down_w[:, e0:e1, :, :]).then_inc(weights_in[n], 16)
            sp.dma_start(xT[:, 2 * CT:TOKENS], x_cols[:, 2 * CT:TOKENS]).then_inc(xcols_in, 16)
            sp.dma_start(xr[:, ROWT:, :], rows[:, ROWT:, :]).then_inc(xrows_in, 16)
            for c in range(CHUNKS - 1):
                sp.wait_ge(result_done, ROWT * (c + 1))
                sp.dma_start(out[tokens(c), :].rearrange("(t p) d -> p t d", p=P),
                             result[:, :, :]).then_inc(stored, 16)
            half_tokens = CT // 2
            for i in range(2):
                rows = slice((CHUNKS - 1) * CT + i * half_tokens, (CHUNKS - 1) * CT + (i + 1) * half_tokens)
                sp.wait_ge(result_done, ROWT * (CHUNKS - 1) + (i + 1) * ROWT // 2)
                sp.dma_start(out[rows, :].rearrange("(t p) d -> p t d", p=P),
                             result[:, i * ROWT // 2:(i + 1) * ROWT // 2, :]).then_inc(stored, 16)
            sp.wait_ge(stored, 16 * (CHUNKS + 1))

        @block.tensor
        def _(pe):
            ident = cst[:, C_ID:C_ID + P]

            def project_q(n):
                if n == 1:
                    pe.wait_ge(xcol1_in, 16)
                    pe.wait_ge(probT_sb, SETS)
                else:
                    after(pe, gT_sb, n)
                pe.matmul(query_bank(n)[:, :], pw[:, W_Q:W_Q + P], xT[:, tokens(n)],
                          start=True, stop=True).then_inc(q_mm, 1)

            def project_kv(n):
                if n == 1:
                    pe.wait_ge(o_done, SETS - 1)
                else:
                    after(pe, logit_done, n)
                pe.matmul(m_bank[0:2 * GD, :], pw[:, W_KV:W_KV + 2 * GD], xT[:, tokens(n)],
                          start=True, stop=True).then_inc(kv_mm, 1)

            def scores(n, s):
                if s == 0:
                    pe.wait_ge(q_sb, HPG * (n + 1))
                    pe.wait_ge(k_sb, GROUPS * (n + 1))
                    pe.wait_ge(halo_done, n // CHUNKS_PER_SEQUENCE + 1)
                if n > 0:
                    pe.wait_ge(v_sb, GROUPS * (n + 1))
                    pe.wait_ge(shift_done, SETS * n + s)
                bank = score_bank(n, s)
                for j in range(BPG):
                    at = (s * BPG + j) * QB
                    mm = pe.matmul(bank[:, j * P:(j + 1) * P], qT[:, s * BPG + j, :, :],
                                   kM[:, :, at:at + 2 * QB],
                                   start=True, stop=True)
                mm.then_inc(score_mm, 1)

            def transpose_prob(n, s):
                pe.wait_ge(exp_done, SETS * n + s + 1)
                if n > 0:
                    pe.wait_ge(q_sb, HPG * (n + 1))
                    after(pe, result_done, ROWT * (n - 1))
                    pe.wait_ge(probT_sb, SETS * n + s)
                else:
                    after(pe, probT_sb, s - 1)
                for j in range(BPG):
                    mm = pe.transpose(prob_bank(n, s)[:, j * P:(j + 1) * P],
                                      prob[:, s, j * P:(j + 1) * P], ident)
                mm.then_inc(probT_mm, 1)

            def weigh_values(n, s):
                if s == 0:
                    pe.wait_ge(vbd_done, n + 1)
                    if n > 0:
                        pe.wait_ge(shift_done, SETS * (n + 1))
                elif n > 0:
                    pe.wait_ge(o_done, SETS * n + s)
                else:
                    after(pe, o_done, s - 1)
                pe.wait_ge(probT_sb, SETS * n + s + 1)
                for j in range(BPG):
                    at = (s * BPG + j) * VW
                    mm = pe.matmul(value_bank(n, s)[:, j * P:(j + 1) * P],
                                   probT[:, s % 2, j * P:(j + 1) * P],
                                   vbd[:, at:at + P], start=True, stop=True)
                mm.then_inc(pv_mm, 1)

            def project_out(n, tiles):
                pe.wait_ge(oT_done, ROWT * n + tiles[-1] + 1)
                for j in tiles:
                    pe.matmul(project_bank(n, j)[:, j * P:(j + 1) * P], oT[:, j * P:(j + 1) * P],
                              pw[:, W_O:W_O + D], start=True, stop=True).then_inc(proj_mm, 1)

            def transpose_x2(n, tiles):
                pe.wait_ge(probT_sb, SETS * (n + 1))
                pe.wait_ge(x2_done, ROWT * n + tiles[-1] + 1)
                for j in tiles:
                    pe.transpose(t_bank[:, j * P:(j + 1) * P], x2[:, j, :], ident).then_inc(x2T_mm, 1)

            def route(n):
                pe.wait_ge(x2T_sb, n + 1)
                pe.wait_ge(res_done, ROWT * (n + 1))
                for j in range(ROWT):
                    mm = pe.matmul(router_bank(n)[:, j * P:(j + 1) * P], x2T[:, (n % 2) * CT + j * P:(n % 2) * CT + (j + 1) * P],
                                   pw[:, W_R:W_R + P], start=True, stop=True)
                mm.then_inc(router_mm, 1)

            def transpose_gates(n):
                pe.wait_ge(gparts_done, n + 1)
                pe.wait_ge(x2T_sb, n + 1)
                for j in range(ROWT):
                    mm = pe.transpose(t_bank[0:2 * EXPERTS, j * P:(j + 1) * P],
                                      gparts[:, j, :].bitcast(F32), ident)
                mm.then_inc(gT_mm, 1)

            def broadcast_gate(c, e):
                if e == 0:
                    pe.wait_ge(gT_sb, c + 1)
                after(pe, xg_done, EXPERTS * c + e)
                pe.matmul(s_bank[:, :], gsel[:, e * P:(e + 1) * P], gT[:, slot(c)],
                          start=True, stop=True).then_inc(gcast_mm, 1)

            def triple(into, w_hi, w_lo, m_hi, m_lo, low_ready, count, start, stop):
                pe.matmul(into, w_hi, m_hi, start=start, stop=False)
                pe.matmul(into, w_lo, m_hi, start=False, stop=False)
                pe.wait_ge(low_ready, count)
                return pe.matmul(into, w_hi, m_lo, start=False, stop=stop)

            def first_up(c, t):
                f, k = divmod(t, 2)
                if t == 0:
                    pe.wait_ge(x2hi_done, c + 1)
                if c == 0 and t in FIRST_OF_LOT:
                    pe.wait_ge(weights_lo, FIRST_OF_LOT[t] + 1)
                after(pe, silu_done, TILES * c + t - 1)
                w1 = slice(k * P, (k + 1) * P)
                triple(gate_bank[t % 2][:, :], up_hi[:, f, w1], up_lo[:, f, w1],
                       x2hi[:, slot(c)], x2lo[:, slot(c)], x2lo_done, c + 1, True, True).then_inc(gate_mm, 1)

            def second_up(c, t):
                f, k = divmod(t, 2)
                w2 = slice(HIDDEN + k * P, HIDDEN + (k + 1) * P)
                after(pe, h_done, TILES * c + t - 1)
                if c == 0 and t == 0:
                    pe.wait_ge(q_sb, 2 * HPG)
                if f == 0:
                    triple(up_bank[t % 2][:, :], up_hi[:, f, w2], up_lo[:, f, w2], x2hi[:, slot(c)],
                           x2lo[:, slot(c)], x2lo_done, c + 1, True, True).then_inc(up_mm, 1)
                else:
                    pe.wait_ge(xghi_done, EXPERTS * c + f)
                    triple(up_bank[t % 2][:, :], up_hi[:, f, w2], up_lo[:, f, w2], xghi[:, (f - 1) % 2, :],
                           xglo[:, (f - 1) % 2, :], xglo_done, EXPERTS * c + f, True, True).then_inc(up_mm, 1)

            def down(c, t):
                f, k = divmod(t, 2)
                if t == 0:
                    after(pe, ysum_done, ROWT * c)
                at = TILES * c + t
                pe.wait_ge(hhi_done, at + 1)
                triple(y_bank[:, :], down_hi[:, f, k, :], down_lo[:, f, k, :],
                       hhi[:, at % RING, :], hlo[:, at % RING, :], hlo_done, at + 1,
                       t == 0, t == TILES - 1).then_inc(down_mm, 1)

            def transpose_result(c, tiles):
                pe.wait_ge(ysum_done, ROWT * c + tiles[-1] + 1)
                pe.wait_ge(q_sb, HPG * min(c + 3, CHUNKS))
                pe.wait_ge(gT_sb, min(c + 2, CHUNKS))
                for j in tiles:
                    pe.transpose(result_bank(c, j)[:, j * P:(j + 1) * P], ysum[:, j * P:(j + 1) * P],
                                 ident).then_inc(yT_mm, 1)

            def beside(c, place):
                n = c + 1
                if place == RESULT_AT and c > 0:
                    transpose_result(c - 1, range(ROWT))
                if n < CHUNKS:
                    if place == KV_AT and n > 1:
                        project_kv(n)
                    if place == Q_AT and n > 1:
                        project_q(n)
                    if place in SCORE_AT:
                        scores(n, SCORE_AT.index(place))
                    if place in PROB_AT:
                        transpose_prob(n, PROB_AT.index(place))
                    if place in VALUE_AT:
                        weigh_values(n, VALUE_AT.index(place))
                    if place == PROJECT_AT:
                        project_out(n, range(ROWT))
                    if place == X2T_AT:
                        transpose_x2(n, range(ROWT))
                    if place == ROUTE_AT:
                        route(n)
                    if place == GATES_AT:
                        transpose_gates(n)
                if c == 0 and place == GATES_0_AT:
                    transpose_gates(0)
                if place in GATED_AT:
                    broadcast_gate(c, GATED_AT.index(place))

            pe.wait_ge(idle_done, 1)
            for _ in range(WARM_UP):
                pe.matmul(y_bank[:, :], idle[:, 0:P], idle[:, :], start=True, stop=True)

            pe.wait_ge(qkv_in, 16)
            pe.wait_ge(xcol0_in, 16)
            project_q(0)
            project_kv(0)
            pe.wait_ge(setup_done, SETUP_STEPS)
            pe.wait_ge(even_picks_done, 1)
            pe.wait_ge(odd_picks_done, 1)
            scores(0, 0)
            scores(0, 1)
            scores(0, 2)
            transpose_prob(0, 0)
            scores(0, 3)
            transpose_prob(0, 1)
            weigh_values(0, 0)
            transpose_prob(0, 2)
            weigh_values(0, 1)
            pe.wait_ge(proj_in, 16)
            project_out(0, [0])
            transpose_prob(0, 3)
            weigh_values(0, 2)
            project_out(0, [1])
            weigh_values(0, 3)
            project_q(1)
            project_out(0, [2])
            project_kv(1)
            project_out(0, [3])
            for j in range(ROWT):
                transpose_x2(0, [j])
            route(0)
            pe.wait_ge(xcols_in, 16)
            for c in range(CHUNKS):
                for t in range(TILES):
                    first_up(c, t)
                    beside(c, (t, 0))
                    second_up(c, t)
                    beside(c, (t, 1))
                    if t >= LAG:
                        down(c, t - LAG)
                    elif c > 0:
                        down(c - 1, TILES + t - LAG)
                    beside(c, (t, 2))
            for t in range(TILES - LAG, TILES):
                down(CHUNKS - 1, t)
            for j in range(ROWT):
                transpose_result(CHUNKS - 1, [j])

        @block.scalar
        def _(act):
            act.dma_start(bias[:, :], biases).then_inc(const_in, 16)
            act.dma_start(cst[:, :], consts).then_inc(const_in, 16)
            act.dma_start(kM[GD:MROWS, :, :], masks).then_inc(mask_in, 16)
            act.dma_start(gsel_f, selectors).then_inc(gsel_in, 16)

            def queries(n):
                bank = query_bank(n)
                act.wait_ge(q_mm, n + 1)
                after(act, score_mm, SETS * n)
                for i in range(HPG):
                    rows = slice(GD * i, GD * (i + 1))
                    act.activation(qT[0:GD, :, i, :], blocks(bank[rows, :], QB), ACT.Identity,
                                   bias=bias[rows, B_Q:B_Q + 1]).then_inc(q_sb, 1)

            def exps(n, s):
                act.wait_ge(shift_done, SETS * n + s + 1)
                act.activation(prob[:, s, :], shifted[:, s, :], ACT.Exp, scale=SCALE).then_inc(exp_done, 1)
                act.activation(esink[:, s, :], mrow[:, s, :], ACT.Exp, scale=-SCALE,
                               bias=bias[:, B_SINK:B_SINK + 1]).then_inc(esink_done, 1)

            def exps_together(n):
                act.wait_ge(shift_done, SETS * (n + 1))
                act.activation(prob[:, :, :], shifted[:, :, :], ACT.Exp, scale=SCALE).then_inc(exp_done, SETS)
                act.activation(esink[:, :, :], mrow[:, :, :], ACT.Exp, scale=-SCALE,
                               bias=bias[:, B_SINK:B_SINK + 1]).then_inc(esink_done, SETS)

            def own_values(n):
                act.wait_ge(v_sb, GROUPS * (n + 1))
                after(act, vbd_done, n)
                for g in range(GROUPS):
                    rows = 2 * g * GD
                    act.activation(vT[rows + GD:rows + 2 * GD, 0:CT], vT[rows:rows + GD, QB:QB + CT],
                                   ACT.Copy).then_inc(own_v_sb, 1)

            def prob_out(n, s):
                act.wait_ge(probT_mm, SETS * n + s + 1)
                after(act, pv_mm, SETS * n + max(s - 1, 0))
                act.activation(probT[:, s % 2, :], prob_bank(n, s)[:, :], ACT.Copy).then_inc(probT_sb, 1)

            def x2T_out(n):
                act.wait_ge(x2T_mm, ROWT * (n + 1))
                after(act, ysum_done, ROWT * (n - 1))
                act.activation(x2T[:, slot(n)], t_bank[:, :], ACT.Copy).then_inc(x2T_sb, 1)

            def router_tanh(n):
                act.wait_ge(lead_done, n + 1)
                act.activation(half[:, :], lead[:, :], ACT.Tanh, scale=0.5).then_inc(half_done, 1)

            def gates_out(n):
                act.wait_ge(gT_mm, n + 1)
                act.activation(gT[:, slot(n)], t_bank[0:2 * EXPERTS, :], ACT.Copy).then_inc(gT_sb, 1)

            def weights_out(lot):
                e0, e1 = WEIGHT_LOTS[lot]
                act.wait_ge(weights_in[lot], 32)
                act.activation(up_hi[:, e0:e1, :], up_f[:, e0:e1, :], ACT.Copy)
                act.activation(down_hi[:, e0:e1, :, :], down_f[:, e0:e1, :, :], ACT.Copy).then_inc(weights_hi, 1)

            def silu(c, t):
                at = TILES * c + t
                act.wait_ge(gate_mm, at + 1)
                after(act, h_done, at - 1)
                act.activation(sil[:, t % 2, :], gate_bank[t % 2][:, :], ACT.Silu).then_inc(silu_done, 1)

            def h_high(at):
                act.wait_ge(h_done, at + 1)
                after(act, down_mm, at - RING + 1)
                act.activation(hhi[:, at % RING, :], h[:, at % 2, :], ACT.Copy).then_inc(hhi_done, 1)

            def xg_high(c, e):
                act.wait_ge(xg_done, EXPERTS * c + e + 1)
                after(act, up_mm, TILES * c + (2 * e if e >= 2 else 0))
                act.activation(xghi[:, e % 2, :], xg[:, slot(e)], ACT.Copy).then_inc(xghi_done, 1)

            def beside(c, place):
                n = c + 1
                if n < CHUNKS:
                    if place == QUERIES_AT and n > 1:
                        queries(n)
                    if place == OWN_VALUES_AT:
                        own_values(n)
                    if place == EXP_AT:
                        exps_together(n)
                    if place in PROB_OUT_AT:
                        prob_out(n, PROB_OUT_AT.index(place))
                    if place == X2T_OUT_AT:
                        x2T_out(n)
                    if place == TANH_AT:
                        router_tanh(n)
                    if place == GATES_OUT_AT:
                        gates_out(n)
                if c == 0 and place == GATES_0_AT:
                    gates_out(0)
                if place in GATED_HIGH_AT:
                    xg_high(c, GATED_HIGH_AT.index(place))
                if c == 0 and place in SPLIT_AT:
                    weights_out(2 + SPLIT_AT.index(place))

            act.wait_ge(exponent_done, 1)
            act.activation(warm[:, :], eps[:, :], ACT.Exp)
            act.wait_ge(const_in, 32)
            act.wait_ge(picks_cleared, 1)
            act.activation(qT[GD:GD + QB, 0::2, :, :], cst[GD:GD + QB, GD:GD + QB].unsqueeze(1).unsqueeze(1)
                           .to_broadcast([QB, BLOCKS // 2, HPG, QB]), ACT.Copy).then_inc(even_picks_done, 1)
            queries(0)
            own_values(0)
            exps(0, 0)
            exps(0, 1)
            prob_out(0, 0)
            exps(0, 2)
            prob_out(0, 1)
            exps(0, 3)
            prob_out(0, 2)
            weights_out(0)
            prob_out(0, 3)
            weights_out(1)
            queries(1)
            x2T_out(0)
            router_tanh(0)
            for c in range(CHUNKS):
                for t in range(TILES):
                    silu(c, t)
                    beside(c, (t, 0))
                    if c + t > 0:
                        h_high(TILES * c + t - 1)
                    beside(c, (t, 1))
                    beside(c, (t, 2))
            h_high(TILES * CHUNKS - 1)

        @block.vector
        def _(dve):
            def keys(n):
                after(dve, score_mm, SETS * n)
                if n > 0:
                    dve.tensor_copy(kM[0:GD + QB, :, 0:QB], kM[0:GD + QB, :, CT:CT + QB]).then_inc(k_carried, 1)
                    dve.wait_ge(k_carried, n)
                if n % CHUNKS_PER_SEQUENCE == 0:
                    dve.memset(kM[GD:GD + QB, :, 0:QB], MASKED).then_inc(halo_done, 1)
                dve.wait_ge(kv_mm, n + 1)
                for g in range(GROUPS):
                    dve.tensor_scalar(kM[0:GD, g, QB:QB + CT], m_bank[0:GD, :], bias[0:GD, B_KV:B_KV + 1],
                                      cst[0:GD, C_GROUP + g:C_GROUP + g + 1],
                                      ALU.add, ALU.mult).then_inc(k_sb, 1)

            def values(n):
                if n > 0:
                    dve.wait_ge(vbd_done, n)
                    for g in range(GROUPS):
                        rows = slice(2 * g * GD, (2 * g + 1) * GD)
                        dve.tensor_copy(vT[rows, 0:QB], vT[rows, CT:CT + QB]).then_inc(v_carried, 1)
                    dve.wait_ge(v_carried, GROUPS * n)
                here = slice(GD, 2 * GD)
                for g in range(GROUPS):
                    dve.tensor_scalar(vT[2 * g * GD:(2 * g + 1) * GD, QB:QB + CT], m_bank[here, :],
                                      bias[here, B_KV:B_KV + 1], cst[here, C_GROUP + g:C_GROUP + g + 1],
                                      ALU.add, ALU.mult).then_inc(v_sb, 1)

            def value_blocks(n):
                dve.wait_ge(v_sb, GROUPS * (n + 1))
                dve.wait_ge(own_v_sb, GROUPS * (n + 1))
                after(dve, pv_mm, SETS * n)
                dve.transpose(blocks(vbd[:, 0:BLOCKS * VW], VW)[:, :, 0:GD],
                              blocks(vT[:, 0:CT], QB)).then_inc(vbd_done, 1)

            def softmax_shift(n, s):
                at = SETS * n + s + 1
                by_row = "p (i k) -> p i k"
                dve.wait_ge(score_mm, at)
                dve.tensor_reduce(mx[:, s, :], score_bank(n, s)[:, :].rearrange(by_row, k=2 * QB),
                                  AX.X, ALU.max).then_inc(max_done, 1)
                dve.wait_ge(max_done, at)
                dve.tensor_scalar(mrow[:, s, :], mx[:, s, :], sink4[:, :], None, ALU.max).then_inc(mrow_done, 1)
                dve.wait_ge(mrow_done, at)
                dve.tensor_tensor(shifted[:, s, :].rearrange(by_row, k=2 * QB),
                                  score_bank(n, s)[:, :].rearrange(by_row, k=2 * QB),
                                  mrow[:, s, :].unsqueeze(2).to_broadcast([P, BPG * GROUPS, 2 * QB]),
                                  ALU.subtract).then_inc(shift_done, 1)

            def normalise(n, s):
                at = SETS * n + s + 1
                weighed = blocks(value_bank(n, s)[:, :], P)
                by_group = "p (b g) -> p b g"
                dve.wait_ge(esink_done, at)
                dve.wait_ge(pv_mm, at)
                dve.tensor_tensor(den[:, s, :].rearrange(by_group, b=BPG), weighed[:, :, GD:VW],
                                  esink[:, s, :].rearrange(by_group, b=BPG), ALU.add).then_inc(den_done, 1)
                dve.wait_ge(den_done, at)
                dve.reciprocal(rden[:, s, :], den[:, s, :]).then_inc(rden_done, 1)
                dve.wait_ge(rden_done, at)
                dve.tensor_tensor(o[:, sets[s]].rearrange("p (b g d) -> p b g d", b=BPG, g=GROUPS),
                                  weighed[:, :, 0:GD].rearrange("p b (g d) -> p b g d", g=GROUPS),
                                  rden[:, s, :].rearrange(by_group, b=BPG).unsqueeze(3)
                                  .to_broadcast([P, BPG, GROUPS, HD]), ALU.mult).then_inc(o_done, 1)

            def turn(n, tiles):
                some = slice(tiles[0] * P, (tiles[-1] + 1) * P)
                dve.wait_ge(o_done, SETS * n + tiles[-1] + 1)
                after(dve, proj_mm, ROWT * n)
                dve.transpose(oT[:, some], o[:, some]).then_inc(oT_done, len(tiles))

            def norm1(n, tiles):
                at = ROWT * n + tiles[-1] + 1
                some = slice(tiles[0], tiles[-1] + 1)
                dve.wait_ge(proj_mm, at)
                dve.wait_ge(xbias_done, 1 if n == 0 else 2)
                dve.tensor_tensor(res[:, some, :], blocks(project_bank(n, tiles[0])[:, :], D)[:, some, :],
                                  xr[:, n * ROWT + tiles[0]:n * ROWT + tiles[-1] + 1, :],
                                  ALU.add).then_inc(res_done, len(tiles))
                dve.wait_ge(res_done, at)
                for j in tiles:
                    dve.bn_stats(bn1[:, j, :], res[:, j, :]).then_inc(bn1_done, 1)
                dve.wait_ge(bn1_done, at)
                for j in tiles:
                    dve.bn_aggr(mv1[:, j, :], bn1[:, j, :]).then_inc(mv1_done, 1)

            def scale1(n, tiles):
                dve.wait_ge(rstd1_done, ROWT * n + tiles[-1] + 1)
                for j in tiles:
                    dve.tensor_scalar(x2[:, j, :], res[:, j, :], mv1[:, j, 0:1], rstd1[:, j:j + 1],
                                      ALU.subtract, ALU.mult).then_inc(x2_done, 1)

            def x2_high(n):
                dve.wait_ge(x2T_sb, n + 1)
                dve.tensor_copy(x2hi[:, slot(n)], x2T[:, slot(n)]).then_inc(x2hi_done, 1)

            def logits(n):
                every = [P, ROWT, EXPERTS]
                dve.wait_ge(router_mm, n + 1)
                dve.tensor_tensor(logit[:, :, :], blocks(router_bank(n)[:, :], P)[:, :, 0:EXPERTS],
                                  bias[:, B_R:B_R + EXPERTS].unsqueeze(1).to_broadcast(every),
                                  ALU.add).then_inc(logit_done, 1)
                dve.wait_ge(logit_done, n + 1)
                for j in range(ROWT):
                    ins = dve.max(top[:, j, :], logit[:, j, :])
                ins.then_inc(top_done, 1)
                dve.wait_ge(top_done, n + 1)
                dve.tensor_tensor(lead[:, :], top[:, :, 0], top[:, :, 1], ALU.subtract).then_inc(lead_done, 1)
                for j in range(ROWT):
                    ins = dve.max_index(topi[:, j, :], top[:, j, :], logit[:, j, :])
                ins.then_inc(topi_done, 1)
                dve.wait_ge(topi_done, n + 1)
                dve.tensor_copy(topf[:, :, :], topi[:, :, 0:2]).then_inc(topf_done, 1)
                dve.wait_ge(topf_done, n + 1)
                for i in range(2):
                    ins = dve.tensor_tensor(pick[:, i, :, :],
                                            cst[:, C_IOTA:C_IOTA + EXPERTS].unsqueeze(1).to_broadcast(every),
                                            topf[:, :, i:i + 1].to_broadcast(every), ALU.is_equal)
                ins.then_inc(pick_done, 1)
                dve.wait_ge(pick_done, n + 1)
                dve.tensor_tensor(signed[:, :, :], pick[:, 0, :, :], pick[:, 1, :, :], ALU.subtract)
                dve.tensor_tensor(picked[:, :, :], pick[:, 0, :, :], pick[:, 1, :, :], ALU.add)\
                   .then_inc(picked_done, 1)
                dve.wait_ge(picked_done, n + 1)
                dve.tensor_scalar(picked[:, :, :], picked[:, :, :], 0.5, None, ALU.mult).then_inc(halved_done, 1)

            def gates(n):
                every = [P, ROWT, EXPERTS]
                dve.wait_ge(half_done, n + 1)
                dve.wait_ge(halved_done, n + 1)
                dve.tensor_tensor(swing[:, :, :], signed[:, :, :], half[:, :].unsqueeze(2).to_broadcast(every),
                                  ALU.mult).then_inc(swing_done, 1)
                dve.wait_ge(swing_done, n + 1)
                dve.scalar_tensor_tensor(gate[:, :, :], swing[:, :, :], 0.5, picked[:, :, :],
                                         ALU.mult, ALU.add).then_inc(gate_done, 1)
                dve.wait_ge(gate_done, n + 1)
                dve.tensor_copy(gparts[:, :, 0:EXPERTS], gate[:, :, :]).then_inc(ghi_done, 1)
                dve.wait_ge(ghi_done, n + 1)
                dve.tensor_tensor(gparts[:, :, EXPERTS:2 * EXPERTS], gate[:, :, :],
                                  gparts[:, :, 0:EXPERTS].bitcast(F32), ALU.subtract).then_inc(gparts_done, 1)

            def gated_input(c, e):
                dve.wait_ge(gcast_mm, EXPERTS * c + e + 1)
                after(dve, xglo_done, EXPERTS * c + e - 1)
                dve.tensor_tensor(xg[:, slot(e)], x2T[:, slot(c)], s_bank[:, :], ALU.mult)\
                   .then_inc(xg_done, 1)

            def xg_low(c, e):
                dve.wait_ge(xghi_done, EXPERTS * c + e + 1)
                dve.wait_ge(xglo_done, EXPERTS * c + e)
                dve.tensor_tensor(xglo[:, e % 2, :], xg[:, slot(e)], xghi[:, e % 2, :].bitcast(F32),
                                  ALU.subtract).then_inc(xglo_done, 1)

            def h_low(at):
                dve.wait_ge(hhi_done, at + 1)
                dve.wait_ge(hlo_done, at)
                dve.tensor_tensor(hlo[:, at % RING, :], h[:, at % 2, :], hhi[:, at % RING, :].bitcast(F32),
                                  ALU.subtract).then_inc(hlo_done, 1)

            def hidden(c, t):
                at = TILES * c + t
                dve.wait_ge(silu_done, at + 1)
                dve.wait_ge(up_mm, at + 1)
                after(dve, hlo_done, at - 1)
                dve.tensor_tensor(h[:, t % 2, :], sil[:, t % 2, :], up_bank[t % 2][:, :], ALU.mult)\
                   .then_inc(h_done, 1)

            def sum_y(c, tiles):
                some = slice(tiles[0] * P, (tiles[-1] + 1) * P)
                dve.wait_ge(down_mm, TILES * (c + 1))
                after(dve, yT_mm, ROWT * c)
                dve.tensor_tensor(ysum[:, some], x2T[:, slot(c)][:, some], y_bank[:, some],
                                  ALU.add).then_inc(ysum_done, len(tiles))

            def stats2(c, tiles):
                at = ROWT * c + tiles[-1] + 1
                dve.wait_ge(yT_mm, at)
                for j in tiles:
                    dve.bn_stats(bn2[:, j, :], result_bank(c, j)[:, j * D:(j + 1) * D]).then_inc(bn2_done, 1)
                dve.wait_ge(bn2_done, at)
                for j in tiles:
                    dve.bn_aggr(mv2[:, j, :], bn2[:, j, :]).then_inc(mv2_done, 1)

            def scale2(c, tiles):
                dve.wait_ge(rstd2_done, ROWT * c + tiles[-1] + 1)
                after(dve, stored, 16 * c)
                for j in tiles:
                    dve.tensor_scalar(result[:, j, :], result_bank(c, j)[:, j * D:(j + 1) * D],
                                      mv2[:, j, 0:1], rstd2[:, j:j + 1],
                                      ALU.subtract, ALU.mult).then_inc(result_done, 1)

            def weights_low(lot):
                e0, e1 = WEIGHT_LOTS[lot]
                dve.wait_ge(weights_hi, lot + 1)
                dve.wait_ge(weights_lo, lot)
                dve.tensor_tensor(up_lo[:, e0:e1, :], up_f[:, e0:e1, :], up_hi[:, e0:e1, :].bitcast(F32),
                                  ALU.subtract)
                dve.tensor_tensor(down_lo[:, e0:e1, :, :], down_f[:, e0:e1, :, :],
                                  down_hi[:, e0:e1, :, :].bitcast(F32), ALU.subtract).then_inc(weights_lo, 1)

            def beside(c, place):
                n = c + 1
                if n < CHUNKS:
                    if place == KEYS_AT and n > 1:
                        keys(n)
                    if place == VALUES_AT:
                        values(n)
                    if place == VBD_AT:
                        value_blocks(n)
                    if place in SHIFT_AT:
                        softmax_shift(n, SHIFT_AT.index(place))
                    if place in NORMALISE_AT:
                        normalise(n, NORMALISE_AT.index(place))
                    if place == TURN_AT:
                        turn(n, range(ROWT))
                    if place == NORM_AT:
                        norm1(n, range(ROWT))
                    if place == SCALE_AT:
                        scale1(n, range(ROWT))
                    if place == X2_HIGH_AT:
                        x2_high(n)
                    if place == PICK_AT:
                        logits(n)
                    if place == WEIGHT_AT:
                        gates(n)
                gated = GATED_INPUT_AT if c > 0 else [GATED_INPUT_0_AT] + GATED_INPUT_AT[1:]
                if place in gated:
                    gated_input(c, gated.index(place))
                if place == STATS_AT and c > 0:
                    stats2(c - 1, range(ROWT))
                if place == STORE_AT and c > 0:
                    scale2(c - 1, range(ROWT))
                if c == 0 and place in SPLIT_LOW_AT:
                    weights_low(2 + SPLIT_LOW_AT.index(place))

            dve.memset(vbd[:, :], 0.0).then_inc(setup_done, 1)
            dve.memset(kM[0:GD, :, 0:QB], 0.0).then_inc(setup_done, 1)
            dve.memset(vT[:, :], 0.0).then_inc(setup_done, 1)
            dve.wait_ge(const_in, 32)
            dve.tensor_scalar(sink4[:, :], bias[:, B_SINK:B_SINK + 1], FP16_MIN, 1.0 / SCALE,
                              ALU.max, ALU.mult).then_inc(setup_done, 1)
            dve.wait_ge(setup_done, 3)
            dve.tensor_copy(blocks(vbd[:, 0:BLOCKS * VW], VW)[:, :, GD:VW],
                            cst[:, C_DEN:C_DEN + GROUPS].unsqueeze(1).to_broadcast([P, BLOCKS, GROUPS]))\
               .then_inc(setup_done, 1)
            dve.wait_ge(gsel_in, 16)
            dve.tensor_copy(gsel[:, :], gsel_f).then_inc(setup_done, 1)
            dve.wait_ge(mask_in, 16)
            keys(0)
            dve.wait_ge(setup_done, SETUP_STEPS)
            values(0)
            softmax_shift(0, 0)
            softmax_shift(0, 1)
            value_blocks(0)
            softmax_shift(0, 2)
            softmax_shift(0, 3)
            normalise(0, 0)
            turn(0, [0])
            for s in range(1, SETS):
                normalise(0, s)
                turn(0, [s])
                norm1(0, [s - 1])
            norm1(0, [ROWT - 1])
            for j in range(ROWT):
                scale1(0, [j])
            x2_high(0)
            dve.wait_ge(x2hi_done, 1)
            dve.tensor_tensor(x2lo[:, slot(0)], x2T[:, slot(0)], x2hi[:, slot(0)].bitcast(F32),
                              ALU.subtract).then_inc(x2lo_done, 1)
            logits(0)
            gates(0)
            keys(1)
            for c in range(CHUNKS):
                for t in range(TILES):
                    if t == LAG and c > 0:
                        sum_y(c - 1, range(ROWT))
                    beside(c, (t, 0))
                    hidden(c, t)
                    beside(c, (t, 1))
                    beside(c, (t, 2))
                    if c == CHUNKS - 1 and (t, 0) in GATED_LOW_AT:
                        xg_low(c, GATED_LOW_AT.index((t, 0)))
                    if TILES * c + t > HURRY_FROM:
                        h_low(TILES * c + t - 1)
            h_low(TILES * CHUNKS - 1)
            for j in range(ROWT):
                sum_y(CHUNKS - 1, [j])
            for j in range(ROWT):
                stats2(CHUNKS - 1, [j])
            for j in range(ROWT):
                scale2(CHUNKS - 1, [j])

        @block.gpsimd
        def _(pool):
            def rstd1_of(n, tiles):
                at = ROWT * n + tiles[-1] + 1
                some = slice(tiles[0], tiles[-1] + 1)
                pool.wait_ge(mv1_done, at)
                pool.tensor_tensor(vareps1[:, some], mv1[:, some, 1], eps[:, some], ALU.add)\
                    .then_inc(vareps1_done, len(tiles))
                pool.wait_ge(vareps1_done, at)
                pool.tensor_tensor(rstd1[:, some], vareps1[:, some], exponent[:, some], ALU.pow)\
                    .then_inc(rstd1_done, len(tiles))

            def rstd2_of(c, tiles):
                at = ROWT * c + tiles[-1] + 1
                some = slice(tiles[0], tiles[-1] + 1)
                pool.wait_ge(mv2_done, at)
                pool.tensor_tensor(vareps2[:, some], mv2[:, some, 1], eps[:, some], ALU.add)\
                    .then_inc(vareps2_done, len(tiles))
                pool.wait_ge(vareps2_done, at)
                pool.tensor_tensor(rstd2[:, some], vareps2[:, some], exponent[:, some], ALU.pow)\
                    .then_inc(rstd2_done, len(tiles))

            def x2_low(n):
                pool.wait_ge(x2hi_done, n + 1)
                pool.tensor_tensor(x2lo[:, slot(n)], x2T[:, slot(n)], x2hi[:, slot(n)].bitcast(F32),
                                   ALU.subtract).then_inc(x2lo_done, 1)

            def h_low(at):
                pool.wait_ge(hhi_done, at + 1)
                pool.tensor_tensor(hlo[:, at % RING, :], h[:, at % 2, :], hhi[:, at % RING, :].bitcast(F32),
                                   ALU.subtract).then_inc(hlo_done, 1)

            def xg_low(c, e):
                pool.wait_ge(xghi_done, EXPERTS * c + e + 1)
                pool.tensor_tensor(xglo[:, e % 2, :], xg[:, slot(e)], xghi[:, e % 2, :].bitcast(F32),
                                   ALU.subtract).then_inc(xglo_done, 1)

            def add_bias(first, last):
                some = xr[:, first:last, :]
                pool.tensor_tensor(some, some, bias[:, B_O:B_O + D].unsqueeze(1)
                                   .to_broadcast([P, last - first, D]), ALU.add).then_inc(xbias_done, 1)

            def weights_low(lot):
                e0, e1 = WEIGHT_LOTS[lot]
                pool.wait_ge(weights_hi, lot + 1)
                pool.tensor_tensor(up_lo[:, e0:e1, :], up_f[:, e0:e1, :], up_hi[:, e0:e1, :].bitcast(F32),
                                   ALU.subtract)
                pool.tensor_tensor(down_lo[:, e0:e1, :, :], down_f[:, e0:e1, :, :],
                                   down_hi[:, e0:e1, :, :].bitcast(F32), ALU.subtract).then_inc(weights_lo, 1)

            def beside(c, place):
                n = c + 1
                if place in GATED_LOW_AT and c < CHUNKS - 1:
                    xg_low(c, GATED_LOW_AT.index(place))
                if place == RSTD2_AT and c > 0:
                    rstd2_of(c - 1, range(ROWT))
                if n < CHUNKS:
                    if place == RSTD1_AT:
                        rstd1_of(n, range(ROWT))
                    if place == X2_LOW_AT:
                        x2_low(n)
                if c == 0 and place == RESIDUAL_AT:
                    pool.wait_ge(xrows_in, 16)
                    add_bias(ROWT, CHUNKS * ROWT)

            pool.memset(idle[:, :], 0.0).then_inc(idle_done, 1)
            pool.memset(eps[:, :], LN_EPS).then_inc(exponent_done, 1)
            pool.memset(exponent[:, :], -0.5).then_inc(exponent_done, 1)
            pool.wait_ge(exponent_done, 2)
            for i in range(2):
                rows = slice(GD + i * QB, GD + (i + 1) * QB)
                pool.memset(qT[rows, :, :, :], 0.0).then_inc(picks_cleared, 1)
                pool.wait_ge(picks_cleared, i + 1)
            pool.wait_ge(const_in, 32)
            pool.tensor_copy(qT[GD + QB:MROWS, 1::2, :, :],
                             cst[GD + QB:MROWS, GD + QB:MROWS].unsqueeze(1).unsqueeze(1)
                             .to_broadcast([QB, BLOCKS // 2, HPG, QB])).then_inc(odd_picks_done, 1)
            pool.wait_ge(odd_picks_done, 1)
            pool.wait_ge(xrow0_in, 16)
            add_bias(0, ROWT)
            pool.wait_ge(exponent_done, 2)
            weights_low(0)
            for j in range(ROWT):
                rstd1_of(0, [j])
            weights_low(1)
            for c in range(CHUNKS):
                for t in range(TILES):
                    if 0 < TILES * c + t <= HURRY_FROM:
                        h_low(TILES * c + t - 1)
                    for place in range(3):
                        beside(c, (t, place))
            for j in range(0, ROWT, 2):
                rstd2_of(CHUNKS - 1, [j, j + 1])


def kernel(L0_attn_x, L0_attn_sink_bias, L0_attn_Wq, L0_attn_bq, L0_attn_Wk, L0_attn_bk, L0_attn_Wv,
           L0_attn_bv, L0_attn_Wo, L0_attn_bo, L0_ffn_sw1, L0_ffn_sw2, L0_ffn_sw3, L0_ffn_ew1,
           L0_ffn_ew2, L0_ffn_ew3, L0_ffn_rw, L0_ffn_rb):
    import numpy as np
    import concourse.bacc as bacc
    from concourse.bass_utils import run_bass_kernel_spmd

    def arr(a):
        return np.asarray(a)

    x = arr(L0_attn_x).reshape(TOKENS, D)

    def rows_by_head(a):
        a = arr(a)
        return a.reshape(GROUPS, HPG, HD, *a.shape[1:]).swapaxes(0, 1).reshape(a.shape)

    router = np.zeros((D, P), np.float32)
    router[:, 0:EXPERTS] = arr(L0_ffn_rw)
    proj = np.concatenate([rows_by_head(L0_attn_Wq).T, arr(L0_attn_Wk).T, arr(L0_attn_Wv).T,
                           rows_by_head(arr(L0_attn_Wo).T), router], axis=1)

    bias = np.zeros((P, B_END), np.float32)
    bias[:, B_Q] = rows_by_head(L0_attn_bq)
    bias[0:2 * GD, B_KV] = np.concatenate([arr(L0_attn_bk), arr(L0_attn_bv)])
    bias[:, B_SINK] = arr(L0_attn_sink_bias)
    bias[:, B_R:B_R + EXPERTS] = arr(L0_ffn_rb)
    bias[:, B_O:B_O + D] = arr(L0_attn_bo)

    up = np.concatenate([np.concatenate([arr(L0_ffn_sw1)[None], arr(L0_ffn_ew1)]),
                         np.concatenate([arr(L0_ffn_sw2)[None], arr(L0_ffn_ew2)])], axis=2)
    up = up.transpose(1, 0, 2)
    down = np.concatenate([arr(L0_ffn_sw3)[None], arr(L0_ffn_ew3)])
    down = down.reshape(FFNS, 2, P, D).transpose(2, 0, 1, 3)

    row = np.arange(P)
    c = np.zeros((P, C_END), np.float32)
    c[:, C_ID:C_ID + P] = np.eye(P)
    c[:, C_IOTA:C_IOTA + EXPERTS] = np.arange(EXPERTS)
    for g in range(GROUPS):
        c[:, C_DEN + g] = row // (2 * QB) == g
        c[:, C_GROUP + g] = (row % GD) // HD == g
    q, k = np.arange(QB)[:, None], np.arange(QB)[None, :]
    before = np.where(k > q, 0.0, MASKED)
    own = np.where(k <= q, 0.0, MASKED)
    even = np.tile(np.concatenate([before, own], axis=1), (1, BLOCKS // 2 + 1))[:, :QB + CT]
    odd = np.tile(np.concatenate([own, before], axis=1), (1, BLOCKS // 2 + 1))[:, :QB + CT]
    mask = np.stack([np.concatenate([even, odd])] * GROUPS, axis=1).astype(np.float32)
    select = np.tile(np.repeat(np.eye(EXPERTS, dtype=np.float32), P, axis=1), (2, 1))

    feeds = {"x_cols": x.T, "x_rows": x, "proj_w": proj, "biases": bias, "consts": c,
             "masks": mask, "selectors": select,
             "up_w": up, "down_w": down}
    feeds = {name: np.ascontiguousarray(a) for name, a in feeds.items()}
    nc = bacc.Bacc("TRN2", target_bir_lowering=False, num_devices=1)
    args = [nc.dram_tensor(name, a.shape, mybir.dt.from_np(a.dtype), kind="ExternalInput").ap()
            for name, a in feeds.items()]
    result = nc.dram_tensor("out", (TOKENS, D), F32, kind="ExternalOutput").ap()
    build(nc, *args, result)
    run = run_bass_kernel_spmd(nc, [feeds], core_ids=[0])
    return run.results[0]["out"].reshape(arr(L0_attn_x).shape)
```
